# Optimizing a Trainium2 kernel written in Bass

```python
import numpy as np
import jax
import jax.numpy as jnp

def _softmax(x, axis=-1):
    return jax.nn.softmax(x, axis=axis)

def _gelu(x):
    return jax.nn.gelu(x, approximate=True)

def _silu(x):
    return jax.nn.silu(x)

def _sigmoid(x):
    return jax.nn.sigmoid(x)

def _layernorm(x, axis=-1, eps=1e-05):
    m = jnp.mean(x, axis=axis, keepdims=True)
    v = jnp.var(x, axis=axis, keepdims=True)
    return (x - m) / jnp.sqrt(v + eps)

def _scatter_add(tgt, idx, src, axis=0):
    return tgt.at[idx].add(src)

def _segment_sum(src, seg, n):
    return jax.ops.segment_sum(src, seg, n)
kernel_name = 'mk_adaln_ffn_d2_seqx_r4_b42dff'

def setup_inputs(seed: int=0):
    np.random.seed(seed)
    _w = jnp.asarray

    def _rec_inputs():
        import jax
        import jax.numpy as jnp
        _rk = jax.random.key(seed)
        x = -0.000125 + 0.9999 * jax.random.normal(jax.random.fold_in(_rk, 1), (4, 512, 512), jnp.float32)
        _lenS = 512 - jax.random.randint(jax.random.fold_in(_rk, 7), (4,), 0, max(1, 512 // 4) + 1, jnp.int32)
        _lenS2 = 512 - jax.random.randint(jax.random.fold_in(_rk, 8), (4,), 0, max(1, 512 // 4) + 1, jnp.int32)
        fside_BxSxS_0 = -1.52775e-05 + 0.999936 * jax.random.normal(jax.random.fold_in(_rk, 11), (4, 512, 512), jnp.float32)
        cond_512 = -5.03954e-05 + 1.00559 * jax.random.normal(jax.random.fold_in(_rk, 12), (4, 128), jnp.float32)
        return (x, fside_BxSxS_0, cond_512)
    x, fside_BxSxS_0, cond_512 = _rec_inputs()

    def _L0_cond_setup():
        import jax, jax.numpy as jnp
        from jax import lax
        import numpy as np
        B, T, C, TD = (8, 512, 512, 128)

        def _bi_wkv(r, k, v, w, u, time_emb):
            tf = jax.nn.sigmoid(jnp.sum(time_emb, axis=-1))[:, None, None]
            decay = jnp.exp(-jnp.exp(w.astype(jnp.float32)))[None, :] * (0.5 + 0.5 * tf[:, :, 0])
            kf = k.astype(jnp.float32)
            vf = v.astype(jnp.float32)
            ek = jnp.exp(jnp.minimum(kf, 30.0))
            ekv = ek * vf

            def step(carry, x):
                a, b = carry
                ekv_t, ek_t = x
                a = a * decay + ekv_t
                b = b * decay + ek_t
                return ((a, b), (a, b))
            ekv_t = jnp.swapaxes(ekv, 0, 1)
            ek_t = jnp.swapaxes(ek, 0, 1)
            init = (jnp.zeros_like(decay), jnp.zeros_like(decay))
            _, (nf, df) = lax.scan(step, init, (ekv_t, ek_t))
            _, (nb, db) = lax.scan(step, init, (ekv_t, ek_t), reverse=True)
            nf = jnp.swapaxes(nf, 0, 1)
            df = jnp.swapaxes(df, 0, 1)
            nb = jnp.swapaxes(nb, 0, 1)
            db = jnp.swapaxes(db, 0, 1)
            euk = jnp.exp(jnp.minimum(u.astype(jnp.float32)[None, None, :] + kf, 30.0))
            num = nf + nb - ekv + euk * vf
            den = df + db - ek + euk
            base = jax.nn.sigmoid(r.astype(jnp.float32)) * (num / jnp.maximum(den, 1e-08))
            out = base * (0.8 + 0.2 * tf)
            return out.astype(r.dtype)
        key = jax.random.key(seed)
        ks = jax.random.split(key, 6)
        return {'r': jax.random.normal(ks[0], (B, T, C), dtype=jnp.float32), 'k': jax.random.normal(ks[1], (B, T, C), dtype=jnp.float32), 'v': jax.random.normal(ks[2], (B, T, C), dtype=jnp.float32), 'w': jax.random.normal(ks[3], (C,), dtype=jnp.float32), 'u': jax.random.normal(ks[4], (C,), dtype=jnp.float32), 'time_emb': jax.random.normal(ks[5], (B, TD), dtype=jnp.float32)}
    _L0_cond_all = _L0_cond_setup()
    _L0_cond_in = {k: v for k, v in _L0_cond_all.items() if k in ('w', 'u')}
    del _L0_cond_all

    def _L0_ffn_setup():
        import jax, jax.numpy as jnp
        import numpy as np
        TOP_K = 8
        key = jax.random.key(seed)
        k1, k2, k3 = jax.random.split(key, 3)
        B, S, H, E = (4, 1024, 512, 64)
        hidden_states = jax.random.normal(k1, (B, S, H), dtype=jnp.float32)
        router_weight = jax.random.normal(k2, (E, H), dtype=jnp.float32)
        router_bias = jnp.zeros((E,), dtype=jnp.float32)
        expert_bias = jax.random.normal(k3, (E, H), dtype=jnp.float32) * 0.1
        return {'hidden_states': hidden_states, 'router_weight': router_weight, 'router_bias': router_bias, 'expert_bias': expert_bias}
    _L0_ffn_all = _L0_ffn_setup()
    _L0_ffn_in = {k: v for k, v in _L0_ffn_all.items() if k in ('router_weight', 'router_bias', 'expert_bias')}
    del _L0_ffn_all

    def _L1_cond_setup():
        import jax, jax.numpy as jnp
        from jax import lax
        import numpy as np
        B, T, C, TD = (8, 512, 512, 128)

        def _bi_wkv(r, k, v, w, u, time_emb):
            tf = jax.nn.sigmoid(jnp.sum(time_emb, axis=-1))[:, None, None]
            decay = jnp.exp(-jnp.exp(w.astype(jnp.float32)))[None, :] * (0.5 + 0.5 * tf[:, :, 0])
            kf = k.astype(jnp.float32)
            vf = v.astype(jnp.float32)
            ek = jnp.exp(jnp.minimum(kf, 30.0))
            ekv = ek * vf

            def step(carry, x):
                a, b = carry
                ekv_t, ek_t = x
                a = a * decay + ekv_t
                b = b * decay + ek_t
                return ((a, b), (a, b))
            ekv_t = jnp.swapaxes(ekv, 0, 1)
            ek_t = jnp.swapaxes(ek, 0, 1)
            init = (jnp.zeros_like(decay), jnp.zeros_like(decay))
            _, (nf, df) = lax.scan(step, init, (ekv_t, ek_t))
            _, (nb, db) = lax.scan(step, init, (ekv_t, ek_t), reverse=True)
            nf = jnp.swapaxes(nf, 0, 1)
            df = jnp.swapaxes(df, 0, 1)
            nb = jnp.swapaxes(nb, 0, 1)
            db = jnp.swapaxes(db, 0, 1)
            euk = jnp.exp(jnp.minimum(u.astype(jnp.float32)[None, None, :] + kf, 30.0))
            num = nf + nb - ekv + euk * vf
            den = df + db - ek + euk
            base = jax.nn.sigmoid(r.astype(jnp.float32)) * (num / jnp.maximum(den, 1e-08))
            out = base * (0.8 + 0.2 * tf)
            return out.astype(r.dtype)
        key = jax.random.key(seed)
        ks = jax.random.split(key, 6)
        return {'r': jax.random.normal(ks[0], (B, T, C), dtype=jnp.float32), 'k': jax.random.normal(ks[1], (B, T, C), dtype=jnp.float32), 'v': jax.random.normal(ks[2], (B, T, C), dtype=jnp.float32), 'w': jax.random.normal(ks[3], (C,), dtype=jnp.float32), 'u': jax.random.normal(ks[4], (C,), dtype=jnp.float32), 'time_emb': jax.random.normal(ks[5], (B, TD), dtype=jnp.float32)}
    _L1_cond_all = _L1_cond_setup()
    _L1_cond_in = {k: v for k, v in _L1_cond_all.items() if k in ('w', 'u')}
    del _L1_cond_all

    def _L1_ffn_setup():
        import jax, jax.numpy as jnp
        import numpy as np
        HIDDEN = 512
        INTER = 1376
        LUT_SIZE = 16

        def _ghost_linear(x, idx, lut):
            w = lut[idx]
            return jnp.einsum('bsh,oh->bso', x, w)
        key = jax.random.key(seed)
        k_x, k_lut, k_g, k_u, k_d = jax.random.split(key, 5)
        x = jax.random.normal(k_x, (2, 1024, HIDDEN), dtype=jnp.float32)
        lut = jax.random.normal(k_lut, (LUT_SIZE,), dtype=jnp.float32) * 0.02
        gate_idx = jax.random.randint(k_g, (INTER, HIDDEN), 0, LUT_SIZE, dtype=jnp.int32)
        up_idx = jax.random.randint(k_u, (INTER, HIDDEN), 0, LUT_SIZE, dtype=jnp.int32)
        down_idx = jax.random.randint(k_d, (HIDDEN, INTER), 0, LUT_SIZE, dtype=jnp.int32)
        return {'x': x, 'lut': lut, 'gate_idx': gate_idx, 'up_idx': up_idx, 'down_idx': down_idx}
    _L1_ffn_all = _L1_ffn_setup()
    _L1_ffn_in = {k: v for k, v in _L1_ffn_all.items() if k in ('lut', 'gate_idx', 'up_idx', 'down_idx')}
    del _L1_ffn_all
    return {'x': x, 'fside_BxSxS_0': fside_BxSxS_0, 'cond_512': cond_512, 'L0_cond_w': _L0_cond_in['w'], 'L0_cond_u': _L0_cond_in['u'], 'L0_ffn_router_weight': _L0_ffn_in['router_weight'], 'L0_ffn_router_bias': _L0_ffn_in['router_bias'], 'L0_ffn_expert_bias': _L0_ffn_in['expert_bias'], 'L1_cond_w': _L1_cond_in['w'], 'L1_cond_u': _L1_cond_in['u'], 'L1_ffn_lut': _L1_ffn_in['lut'], 'L1_ffn_gate_idx': _L1_ffn_in['gate_idx'], 'L1_ffn_up_idx': _L1_ffn_in['up_idx'], 'L1_ffn_down_idx': _L1_ffn_in['down_idx']}

def reference(x, fside_BxSxS_0, cond_512, L0_cond_w, L0_cond_u, L0_ffn_router_weight, L0_ffn_router_bias, L0_ffn_expert_bias, L1_cond_w, L1_cond_u, L1_ffn_lut, L1_ffn_gate_idx, L1_ffn_up_idx, L1_ffn_down_idx):
    import jax
    import jax.numpy as jnp

    def _L0_cond_ref(r, k, v, w, u, time_emb):
        import jax, jax.numpy as jnp
        from jax import lax
        import numpy as np
        B, T, C, TD = (8, 512, 512, 128)

        def _bi_wkv(r, k, v, w, u, time_emb):
            tf = jax.nn.sigmoid(jnp.sum(time_emb, axis=-1))[:, None, None]
            decay = jnp.exp(-jnp.exp(w.astype(jnp.float32)))[None, :] * (0.5 + 0.5 * tf[:, :, 0])
            kf = k.astype(jnp.float32)
            vf = v.astype(jnp.float32)
            ek = jnp.exp(jnp.minimum(kf, 30.0))
            ekv = ek * vf

            def step(carry, x):
                a, b = carry
                ekv_t, ek_t = x
                a = a * decay + ekv_t
                b = b * decay + ek_t
                return ((a, b), (a, b))
            ekv_t = jnp.swapaxes(ekv, 0, 1)
            ek_t = jnp.swapaxes(ek, 0, 1)
            init = (jnp.zeros_like(decay), jnp.zeros_like(decay))
            _, (nf, df) = lax.scan(step, init, (ekv_t, ek_t))
            _, (nb, db) = lax.scan(step, init, (ekv_t, ek_t), reverse=True)
            nf = jnp.swapaxes(nf, 0, 1)
            df = jnp.swapaxes(df, 0, 1)
            nb = jnp.swapaxes(nb, 0, 1)
            db = jnp.swapaxes(db, 0, 1)
            euk = jnp.exp(jnp.minimum(u.astype(jnp.float32)[None, None, :] + kf, 30.0))
            num = nf + nb - ekv + euk * vf
            den = df + db - ek + euk
            base = jax.nn.sigmoid(r.astype(jnp.float32)) * (num / jnp.maximum(den, 1e-08))
            out = base * (0.8 + 0.2 * tf)
            return out.astype(r.dtype)
        return _bi_wkv(r, k, v, w, u, time_emb)

    def _L0_ffn_ref(hidden_states, router_weight, router_bias, expert_bias):
        import jax, jax.numpy as jnp
        import numpy as np
        TOP_K = 8
        B, S, H = hidden_states.shape
        flat = hidden_states.reshape(B * S, H)
        logits = jnp.einsum('th,eh->te', flat, router_weight) + router_bias
        scores = jax.nn.softmax(logits, axis=-1)
        topk_w, topk_idx = jax.lax.top_k(scores, TOP_K)
        gathered_bias = expert_bias[topk_idx]
        out = flat * jnp.sum(topk_w, axis=-1, keepdims=True) + jnp.einsum('tk,tkh->th', topk_w, gathered_bias)
        return out.reshape(B, S, H)

    def _L1_cond_ref(r, k, v, w, u, time_emb):
        import jax, jax.numpy as jnp
        from jax import lax
        import numpy as np
        B, T, C, TD = (8, 512, 512, 128)

        def _bi_wkv(r, k, v, w, u, time_emb):
            tf = jax.nn.sigmoid(jnp.sum(time_emb, axis=-1))[:, None, None]
            decay = jnp.exp(-jnp.exp(w.astype(jnp.float32)))[None, :] * (0.5 + 0.5 * tf[:, :, 0])
            kf = k.astype(jnp.float32)
            vf = v.astype(jnp.float32)
            ek = jnp.exp(jnp.minimum(kf, 30.0))
            ekv = ek * vf

            def step(carry, x):
                a, b = carry
                ekv_t, ek_t = x
                a = a * decay + ekv_t
                b = b * decay + ek_t
                return ((a, b), (a, b))
            ekv_t = jnp.swapaxes(ekv, 0, 1)
            ek_t = jnp.swapaxes(ek, 0, 1)
            init = (jnp.zeros_like(decay), jnp.zeros_like(decay))
            _, (nf, df) = lax.scan(step, init, (ekv_t, ek_t))
            _, (nb, db) = lax.scan(step, init, (ekv_t, ek_t), reverse=True)
            nf = jnp.swapaxes(nf, 0, 1)
            df = jnp.swapaxes(df, 0, 1)
            nb = jnp.swapaxes(nb, 0, 1)
            db = jnp.swapaxes(db, 0, 1)
            euk = jnp.exp(jnp.minimum(u.astype(jnp.float32)[None, None, :] + kf, 30.0))
            num = nf + nb - ekv + euk * vf
            den = df + db - ek + euk
            base = jax.nn.sigmoid(r.astype(jnp.float32)) * (num / jnp.maximum(den, 1e-08))
            out = base * (0.8 + 0.2 * tf)
            return out.astype(r.dtype)
        return _bi_wkv(r, k, v, w, u, time_emb)

    def _L1_ffn_ref(x, lut, gate_idx, up_idx, down_idx):
        import jax, jax.numpy as jnp
        import numpy as np
        HIDDEN = 512
        INTER = 1376
        LUT_SIZE = 16

        def _ghost_linear(x, idx, lut):
            w = lut[idx]
            return jnp.einsum('bsh,oh->bso', x, w)
        gate = _ghost_linear(x, gate_idx, lut)
        up = _ghost_linear(x, up_idx, lut)
        h = jax.nn.silu(gate) * up
        return _ghost_linear(h, down_idx, lut)
    x = x + _L0_ffn_ref(_L0_cond_ref(x, fside_BxSxS_0, fside_BxSxS_0, L0_cond_w, L0_cond_u, cond_512), L0_ffn_router_weight, L0_ffn_router_bias, L0_ffn_expert_bias)
    x = x + _L1_ffn_ref(_L1_cond_ref(x, fside_BxSxS_0, fside_BxSxS_0, L1_cond_w, L1_cond_u, cond_512), L1_ffn_lut, L1_ffn_gate_idx, L1_ffn_up_idx, L1_ffn_down_idx)
    return x

_drawn_inputs = setup_inputs


def setup_inputs(seed=0):
    import zlib

    import numpy as np

    out = dict(_drawn_inputs(seed))
    spreads = {'L0_ffn_router_bias': (0.0, 0.8)}
    factors = {'L0_cond_u': 4.661,
     'L0_ffn_router_weight': 3.381,
     'L0_ffn_expert_bias': 3.36,
     'L1_cond_u': 8.0}
    for name, (base, spread) in spreads.items():
        noise = np.random.default_rng([zlib.crc32(name.encode()), seed]).standard_normal(out[name].shape)
        drawn = base * np.exp(spread * noise) if base else spread * noise
        out[name] = jnp.asarray(drawn.astype(out[name].dtype))
    for name, factor in factors.items():
        out[name] = (out[name] * factor).astype(out[name].dtype)
    return out
```

```python
from contextlib import ExitStack

import concourse.bass as bass
from concourse import mybir

F32 = mybir.dt.float32
F32R = mybir.dt.float32r
I32 = mybir.dt.int32
I16 = mybir.dt.int16
ALU = mybir.AluOpType
ACT = mybir.ActivationFunctionType

P = 128
B, T, C = 4, 512, 512
CC = C // P
E = 64
TT = T // P
F = 1376
FJ = -(-F // P)
FLAST = F - (FJ - 1) * P
WJ = 3 * CC * P
SB = 768
NS = FJ * WJ // SB
HU = 2 * CC
KMAX = 30.0
EXP_KMAX = 1.0686474581524463e13
DEN_MIN = 1e-8
TAKEN = -3.0e38


def build(nc, x, k, cond, w, u, router_w, router_b, expert_b, lut, idx, y):
    ctx = ExitStack()
    with ctx:
        def sb(name, shape, dt=F32, into=ctx):
            return into.enter_context(nc.sbuf_tensor(name, shape, dt))

        def sem(name):
            return ctx.enter_context(nc.semaphore(name))

        x1_dram = nc.dram_tensor("x1_scratch", (B, CC, P, T), F32, kind="Internal").ap()

        wh = sb("wh", [P, FJ, WJ], F32R)
        wl = sb("wl", [P, FJ, WJ], F32R)
        rw = sb("rw", [P, CC, E])
        rb = sb("rb", [P, E])
        eb = sb("eb", [E, C])
        ones = sb("ones", [P, P])
        ident = sb("ident", [P, P])
        cond_t = sb("cond_t", [P, B])
        w_in = sb("w_in", [P, 2 * CC])
        u_in = sb("u_in", [P, 2 * CC])
        tf = sb("tf", [P, 4, B])
        dec0 = sb("dec0", [P, 2, 2 * CC])
        dec = sb("dec", [P, B, 2 * CC])
        osc = sb("osc", [P, B])
        lut_in = sb("lut_in", [P, 16])
        lut_d = sb("lut_d", [P, 8])

        ps_g = ctx.enter_context(nc.psum_tensor("ps_g", [P, T], F32))
        ps_u = ctx.enter_context(nc.psum_tensor("ps_u", [P, T], F32))
        ps_d = [ctx.enter_context(nc.psum_tensor(f"ps_d{c}", [P, T], F32)) for c in range(CC)]
        ps_a = ctx.enter_context(nc.psum_tensor("ps_a", [P, T], F32))
        ps_b = ctx.enter_context(nc.psum_tensor("ps_b", [P, T], F32))

        consts_in = sem("consts_in")
        pool_consts = sem("pool_consts")
        cond_sum = sem("cond_sum")
        setup_exp = sem("setup_exp")
        setup_dve = sem("setup_dve")
        round_done = sem("round_done")
        go = sem("go")
        held = {n: sem(f"held_{n}") for n in ("act", "dve", "pool", "pe")}
        idx_in = [sem("idx_in0"), sem("idx_in1")]
        idx_narrow = sem("idx_narrow")
        bit0_ready = sem("bit0_ready")
        leaves_act = sem("leaves_act")
        leaves_pool = sem("leaves_pool")
        select_chain = sem("select_chain")
        weight_full = sem("weight_full")
        weight_hi = sem("weight_hi")
        weight_lo = sem("weight_lo")
        y_out = sem("y_out")
        names = """k_in0 k_in1 x_in0 x_in1 xb_in0 xb_in1 x1_out0 x1_out1 x1_back cur_ready k_capped ek_ready ekv_ready
            e_ready t0_ready den_scans num_scans den_sum num_sum den_full den_ready lifted num_full ln_done
            recip_done newton quotient ratio_done base0_ready logits_done l0_chain top_done exps_done picked picked_t
            pick_done spread_done mix_done mix_half mixed x1_ready t1_ready base1_ready x_hi x_lo gate_done up_done
            silu_done h_full h_hi h_lo down_done down_used""".split()
        S = {n: sem(n) for n in names}
        nums = sorted(s.num for s in S.values())
        assert nums == list(range(nums[0], nums[0] + len(nums)))
        cleared = range(nums[0], nums[-1] + 1)

        def hold(eng, name, s, value):
            eng.wait_ge(s, value)
            eng.sem_inc(held[name], 1)

        def end_round(eng):
            eng.drain().then_inc(round_done, 1)

        block_lookup(nc, locals())
        block_main(nc, locals())


def block_lookup(nc, v):
    sb = v["sb"]
    (idx, wh, wl, lut_in, lut_d, hold, end_round) = (v[n] for n in "idx wh wl lut_in lut_d hold end_round".split())
    (idx_in, idx_narrow, bit0_ready, leaves_act, leaves_pool, select_chain, weight_full, weight_hi,
     weight_lo) = (v[n] for n in ("idx_in idx_narrow bit0_ready leaves_act leaves_pool select_chain "
                                  "weight_full weight_hi weight_lo").split())
    (consts_in, pool_consts, cond_sum, setup_exp, setup_dve, round_done, go) = (
        v[n] for n in "consts_in pool_consts cond_sum setup_exp setup_dve round_done go".split())
    (cond_t, w_in, u_in, tf, dec0, dec, osc, ones, ident, rw, rb, eb, ps_a) = (
        v[n] for n in "cond_t w_in u_in tf dec0 dec osc ones ident rw rb eb ps_a".split())
    ACT_LEAVES = range(0, 5)
    POOL_LEAVES = range(5, 8)
    with ExitStack() as tmp:
        idx_sb = [sb(f"idx_sb{p}", [P, SB], I32, tmp) for p in range(2)]
        idx16 = sb("idx16", [P, SB], I16, tmp)
        bit = [sb(f"bit{n}", [P, SB], I16, tmp) for n in range(1, 4)]
        bit0 = [sb(f"bit0_{p}", [P, SB], I16, tmp) for p in range(2)]
        leaf = [[sb(f"leaf{p}_{n}", [P, SB], F32, tmp) for n in range(8)] for p in range(2)]
        wh_flat = wh[:, :, :].rearrange("p j n -> p (j n)")
        wl_flat = wl[:, :, :].rearrange("p j n -> p (j n)")
        idx_flat = idx.rearrange("s p n -> (s p) n")
        block = tmp.enter_context(nc.Block())

        @block.sync
        def _(sp):
            for n in ("lut", "cond", "w", "u", "router_w", "router_b", "expert_b"):
                dst = {"lut": lut_in, "cond": cond_t, "w": w_in, "u": u_in, "router_w": rw, "router_b": rb,
                       "expert_b": eb}[n]
                src = v[n]
                if n in ("lut", "router_b"):
                    src = src.to_broadcast([P, src.shape[1]])
                if n == "router_w":
                    sp.dma_start(dst[:, :, :], src).then_inc(consts_in, 16)
                else:
                    sp.dma_start(dst[:, :], src).then_inc(consts_in, 16)
            for s in range(2):
                sp.dma_start(idx_sb[s][:, :], idx[s]).then_inc(idx_in[s], 16)
            with sp.Fori(0, NS // 2 - 1) as it:
                for p in range(2):
                    sp.wait_ge(idx_narrow, 2 * it + p + 1)
                    sp.dma_start(idx_sb[p][:, :], idx_flat[bass.ds((2 * it + p + 2) * P, P), :]).then_inc(idx_in[p], 16)
            sp.wait_ge(round_done, 4)
            sp.sem_clear(round_done)
            sp.sem_inc(go, 1)

        def leaves(eng, p, which, done):
            for n in which:
                if eng is nc.scalar:
                    ins = eng.activation(leaf[p][n][:, :], bit0[p][:, :], ACT.Identity,
                                         bias=lut_in[:, 2 * n:2 * n + 1], scale=lut_d[:, n:n + 1])
                else:
                    ins = eng.tensor_scalar(leaf[p][n][:, :], bit0[p][:, :], lut_d[:, n:n + 1],
                                            lut_in[:, 2 * n:2 * n + 1], ALU.mult, ALU.add)
            ins.then_inc(done, 1)

        @block.scalar
        def _(act):
            act.wait_ge(consts_in, 112)
            act.wait_ge(cond_sum, 1)
            nc.scalar.activation(tf[:, 0, :], ps_a[:, 0:B], ACT.Exp, scale=-1.0).then_inc(setup_exp, 1)
            nc.scalar.activation(dec0[:, 0, :], w_in[:, :], ACT.Exp).then_inc(setup_exp, 1)
            act.wait_ge(setup_exp, 2)
            nc.scalar.activation(dec0[:, 1, :], dec0[:, 0, :], ACT.Exp, scale=-1.0).then_inc(setup_exp, 1)
            act.wait_ge(bit0_ready, 1)
            leaves(nc.scalar, 0, ACT_LEAVES, leaves_act)

            def step(s, p, more):
                if more:
                    hold(act, "act", bit0_ready, s + 2)
                    hold(act, "act", weight_lo, s)
                    leaves(nc.scalar, 1 - p, ACT_LEAVES, leaves_act)
                hold(act, "act", weight_full, s + 1)
                nc.scalar.activation(wh_flat[:, bass.ds(s * SB, SB)], leaf[p][0][:, :],
                                     ACT.Copy).then_inc(weight_hi, 1)

            with act.Fori(0, NS // 2 - 1) as it:
                for p in range(2):
                    step(2 * it + p, p, True)
            step(NS - 2, 0, True)
            step(NS - 1, 1, False)
            end_round(act)

        @block.gpsimd
        def _(pool):
            nc.gpsimd.memset(ones[:, :], 1.0).then_inc(pool_consts, 1)
            nc.gpsimd.memset(ident[:, :], 0.0).then_inc(pool_consts, 1)
            pool.wait_ge(pool_consts, 2)
            nc.gpsimd.affine_select(out=ident[:, :], in_=ident[:, :], compare_op=ALU.not_equal, fill=1.0, base=0,
                                    pattern=[[-1, P]], channel_multiplier=1).then_inc(pool_consts, 1)
            pool.wait_ge(bit0_ready, 1)
            leaves(nc.gpsimd, 0, POOL_LEAVES, leaves_pool)

            def step(s, p, more):
                if more:
                    hold(pool, "pool", bit0_ready, s + 2)
                    hold(pool, "pool", weight_lo, s)
                    leaves(nc.gpsimd, 1 - p, POOL_LEAVES, leaves_pool)
                hold(pool, "pool", weight_hi, s + 1)
                nc.gpsimd.tensor_tensor(wl_flat[:, bass.ds(s * SB, SB)], leaf[p][0][:, :],
                                        wh_flat[:, bass.ds(s * SB, SB)].bitcast(F32), ALU.subtract).then_inc(weight_lo, 1)

            with pool.Fori(0, NS // 2 - 1) as it:
                for p in range(2):
                    step(2 * it + p, p, True)
            step(NS - 2, 0, True)
            step(NS - 1, 1, False)
            end_round(pool)

        @block.tensor
        def _(pe):
            pe.wait_ge(consts_in, 112)
            pe.wait_ge(pool_consts, 3)
            nc.tensor.matmul(ps_a[:, 0:B], ones[:, :], cond_t[:, :], start=True, stop=True).then_inc(cond_sum, 1)
            end_round(pe)

        @block.vector
        def _(dve):
            chain = [0]

            def link(ins):
                chain[0] += 1
                ins.then_inc(setup_dve, 1)
                dve.wait_ge(setup_dve, chain[0])

            dve.wait_ge(consts_in, 112)
            pair = lut_in[:, :].rearrange("p (n two) -> p n two", two=2)
            link(nc.vector.tensor_tensor(lut_d[:, :], pair[:, :, 1], pair[:, :, 0], ALU.subtract))

            def narrow(p, s, part):
                if part == 0:
                    nc.vector.tensor_copy(idx16[:, :], idx_sb[p][:, :]).then_inc(idx_narrow, 1)
                elif part == 1:
                    nc.vector.tensor_scalar(bit0[p][:, :], idx16[:, :], 1, None, ALU.bitwise_and).then_inc(bit0_ready, 1)
                else:
                    return nc.vector.tensor_scalar(bit[part - 2][:, :], idx16[:, :], 1 << (part - 1), None,
                                                   ALU.bitwise_and)

            dve.wait_ge(idx_in[0], 16)
            narrow(0, 0, 0)
            dve.wait_ge(idx_narrow, 1)
            for part in range(1, 5):
                ins = narrow(0, 0, part)
            ins.then_inc(select_chain, 1)
            dve.wait_ge(select_chain, 1)
            dve.sem_clear(select_chain)
            dve.wait_ge(setup_exp, 3)
            link(nc.vector.tensor_scalar(tf[:, 1, :], tf[:, 0, :], 1.0, None, ALU.add))
            link(nc.vector.reciprocal(tf[:, 2, :], tf[:, 1, :]))
            link(nc.vector.tensor_scalar(tf[:, 3, :], tf[:, 2, :], 0.5, 0.5, ALU.mult, ALU.add))
            link(nc.vector.tensor_scalar(osc[:, :], tf[:, 2, :], -0.1, -0.4, ALU.mult, ALU.add))
            for b in range(B):
                link(nc.vector.tensor_scalar(dec[:, b, :], dec0[:, 1, :], tf[:, 3, b:b + 1], None, ALU.mult))

            def select(p, a, bitn):
                return nc.vector.copy_predicated(leaf[p][a][:, :], bit[bitn - 1][:, :], leaf[p][a + (1 << (bitn - 1))][:, :])

            def step(s, p, more):
                if more:
                    hold(dve, "dve", idx_in[1 - p], 16 * ((s + 1) // 2 + 1) if isinstance(s, int) else 16 * (s - p) // 2 + 16 * (1 + p))
                    narrow(1 - p, s, 0)
                hold(dve, "dve", leaves_act, s + 1)
                hold(dve, "dve", leaves_pool, s + 1)
                for a in (0, 2, 4, 6):
                    select(p, a, 1).then_inc(select_chain, 1)
                if more:
                    hold(dve, "dve", idx_narrow, s + 2)
                    narrow(1 - p, s, 1)
                dve.wait_ge(select_chain, 4)
                for a in (0, 4):
                    select(p, a, 2).then_inc(select_chain, 1)
                if more:
                    narrow(1 - p, s, 2).then_inc(select_chain, 1)
                dve.wait_ge(select_chain, 6)
                select(p, 0, 3).then_inc(weight_full, 1)
                if more:
                    dve.wait_ge(select_chain, 7)
                    narrow(1 - p, s, 3).then_inc(select_chain, 1)
                    hold(dve, "dve", weight_full, s + 1)
                    narrow(1 - p, s, 4).then_inc(select_chain, 1)
                    dve.wait_ge(select_chain, 9)
                dve.sem_clear(select_chain)

            with dve.Fori(0, NS // 2 - 1) as it:
                for p in range(2):
                    step(2 * it + p, p, True)
            step(NS - 2, 0, True)
            step(NS - 1, 1, False)
            end_round(dve)


def block_main(nc, v):
    sb, S, hold, end_round = v["sb"], v["S"], v["hold"], v["end_round"]
    (x, k, y, x1_dram, wh, wl, rw, rb, eb, ones, ident, u_in, dec, osc) = (
        v[n] for n in "x k y x1_dram wh wl rw rb eb ones ident u_in dec osc".split())
    ps_g, ps_u, ps_d, ps_a, ps_b = (v[n] for n in "ps_g ps_u ps_d ps_a ps_b".split())
    go, round_done, y_out, cleared = (v[n] for n in "go round_done y_out cleared".split())
    with ExitStack() as tmp:
        def t(name, shape, dt=F32):
            return sb(name, shape, dt, tmp)

        xh = t("xh", [P, CC, T], F32R)
        xl = t("xl", [P, CC, T], F32R)
        base1 = t("base1", [P, CC, T])
        base0 = t("base0", [P, CC, T])
        kb = [t(f"kb{p}", [P, T]) for p in range(2)]
        ek = [t(f"ek{p}", [P, T]) for p in range(2)]
        ekv = [t(f"ekv{p}", [P, T]) for p in range(2)]
        eu = t("eu", [P, T])
        fd = [t(f"fd{p}", [P, T]) for p in range(2)]
        bd = [t(f"bd{p}", [P, T]) for p in range(2)]
        fn = [t(f"fn{p}", [P, T]) for p in range(2)]
        bn = [t(f"bn{p}", [P, T]) for p in range(2)]
        xs = [t(f"xs{p}", [P, T]) for p in range(2)]
        act_h = [t(f"act_h{p}", [P, T]) for p in range(2)]
        hh = [t(f"hh{p}", [P, T], F32R) for p in range(2)]
        hl = [t(f"hl{p}", [P, T], F32R) for p in range(2)]
        dec_cur = t("dec_cur", [P, 2 * CC])
        osc_cur = t("osc_cur", [P, 1])
        top8 = t("top8", [P, TT, 8])
        neg_max = t("neg_max", [P, TT])
        zsum = t("zsum", [P, TT])
        zinv = t("zinv", [P, TT])
        logits = fd[0][:, 0:TT * E].rearrange("p (t e) -> p t e", e=E)
        marked = fd[0][:, TT * E:2 * TT * E].rearrange("p (t e) -> p t e", e=E)
        exps = bd[0][:, 0:TT * E].rearrange("p (t e) -> p t e", e=E)
        picked = bd[0][:, TT * E:2 * TT * E].rearrange("p (t e) -> p t e", e=E)
        picked_t = bn[0][0:E, :]
        x1b = [fd[1], bd[1], fn[1], bn[1]]

        block = tmp.enter_context(nc.Block())

        @block.sync
        def _(sp):
            def body(b, G, R):
                nxt = b + 1
                for i in range(HU + 3):
                    c, layer = divmod(i, 2)
                    if R and layer == 0 and c < CC:
                        if c >= 2:
                            sp.wait_ge(S["lifted"], 2 * (c - 1))
                            sp.wait_ge(S["ekv_ready"], c - 1)
                        sp.dma_start(kb[c % 2][:, :], row(k, nxt, c)).then_inc(S[f"k_in{c % 2}"], 16)
                        if c >= 2:
                            sp.wait_ge(S["base0_ready"], c - 1)
                        sp.dma_start(xs[c % 2][:, :], row(x, nxt, c)).then_inc(S[f"x_in{c % 2}"], 16)
                if R:
                    for c in range(CC):
                        if c < 2:
                            sp.wait_ge(S["base0_ready"], c + 3)
                        else:
                            sp.wait_ge(S[f"x1_out{c % 2}"], 16)
                            sp.wait_ge(S["t1_ready"], c - 1)
                        sp.dma_start(xs[c % 2][:, :], row(x, nxt, c)).then_inc(S[f"xb_in{c % 2}"], 16)
                        if c >= 1:
                            store_x1(sp, nxt, c - 1)
                    store_x1(sp, nxt, CC - 1)
                if G:
                    if R:
                        sp.wait_ge(S["ratio_done"], HU)
                    for c in range(CC):
                        sp.dma_start(x1b[c][:, :], row(x1_dram, b, c)).then_inc(S["x1_back"], 16)
                    for c in range(CC):
                        sp.wait_ge(S["down_used"], c + 1)
                        sp.dma_start(row(y, b, c), x1b[c][:, :]).then_inc(y_out, 16)
                if R:
                    sp.wait_ge(S["x1_out0"], 32)
                    sp.wait_ge(S["x1_out1"], 32)
                sp.wait_ge(round_done, 4)
                sp.sem_clear(cleared)
                sp.sem_clear(round_done)
                sp.sem_inc(go, 1)

            def store_x1(sp, nxt, c):
                sp.wait_ge(S["x1_ready"], c + 1)
                sp.dma_start(row(x1_dram, nxt, c), xs[c % 2][:, :]).then_inc(S[f"x1_out{c % 2}"], 16)

            def row(a, b, c):
                flat = a.rearrange("b c p t -> (b c p) t")
                return flat[bass.ds((b * CC + c) * P, P), :]

            body(-1, False, True)
            with sp.Fori(0, B - 1) as b:
                body(b, True, True)
            body(B - 1, True, False)
            sp.wait_ge(y_out, 16 * B * CC)

        @block.scalar
        def _(act):
            def body(b, G, R):
                hold(act, "act", go, b + 2)
                for j in range(FJ + 1):
                    c, layer = divmod(j, 2)
                    rec = R and j < HU
                    if G and j >= 1:
                        act.wait_ge(S["h_full"], j)
                        if j >= 3:
                            act.wait_ge(S["down_done"], j - 2)
                        nc.scalar.activation(hh[(j - 1) % 2][:, :], act_h[(j - 1) % 2][:, :],
                                             ACT.Copy).then_inc(S["h_hi"], 1)
                    if rec:
                        if j == 0:
                            nc.scalar.preload_act_table_set("natural_log_exp_and_others")
                            ek_of(0)
                        if layer == 0:
                            act.wait_ge(S[f"k_in{c % 2}"], 16 * (c // 2 + 1))
                        if j >= 1:
                            act.wait_ge(S["num_full"], j)
                            act.wait_ge(S["den_ready"], j)
                        n = layer * CC + c
                        nc.scalar.activation(eu[:, :], kb[c % 2][:, :], ACT.Exp,
                                             bias=u_in[:, n:n + 1]).then_inc(S["e_ready"], 1)
                        if layer == 1 and c + 1 < CC:
                            ek_of(c + 1)
                    if R and j == 8:
                        act.wait_ge(S["top_done"], 1)
                        for n in range(TT):
                            ins = nc.scalar.activation(exps[:, n, :], logits[:, n, :], ACT.Exp,
                                                       bias=neg_max[:, n:n + 1], accum_out=zsum[:, n:n + 1])
                        ins.then_inc(S["exps_done"], 1)
                    if R and j == 9:
                        act.wait_ge(S["pick_done"], 1)
                        nc.scalar.activation(picked_t, ps_b[0:E, :], ACT.Copy).then_inc(S["picked_t"], 1)
                    if G and j < FJ:
                        act.wait_ge(S["gate_done"], j + 1)
                        if j >= 2:
                            act.wait_ge(S["h_lo"], j - 1)
                        nc.scalar.activation(act_h[j % 2][:, :], ps_g[:, :], ACT.Silu).then_inc(S["silu_done"], 1)
                    if rec and layer == 0:
                        act.wait_ge(S[f"x_in{c % 2}"], 16 * (c // 2 + 1))
                        nc.scalar.activation(xs[c % 2][:, :], xs[c % 2][:, :], ACT.Tanh,
                                             scale=0.5).then_inc(S["t0_ready"], 1)
                    if R and j in (9, 10, 11):
                        for c1 in {9: (0,), 10: (1, 2), 11: (3,)}[j]:
                            act.wait_ge(S["x1_ready"], c1 + 1)
                            nc.scalar.activation(base0[:, c1, :], xs[c1 % 2][:, :], ACT.Tanh,
                                                 scale=0.5).then_inc(S["t1_ready"], 1)
                    if rec:
                        nc.scalar.preload_act_table_set("natural_log_exp_and_others")
                        act.wait_ge(S["den_ready"], j + 1)
                        act.wait_ge(S["num_sum"], j + 1)
                        nc.scalar.activation(bn[j % 2][:, :], bd[j % 2][:, :], ACT.Ln).then_inc(S["ln_done"], 1)
                        act.wait_ge(S["ln_done"], j + 1)
                        nc.scalar.activation(bn[j % 2][:, :], bn[j % 2][:, :], ACT.Exp,
                                             scale=-1.0).then_inc(S["recip_done"], 1)
                if R:
                    if G:
                        act.wait_ge(S["up_done"], FJ)
                    for c in range(CC):
                        act.wait_ge(S["base1_ready"], c + 1)
                        nc.scalar.activation(xh[:, c, :], base1[:, c, :], ACT.Copy).then_inc(S["x_hi"], 1)
                end_round(act)

            def ek_of(c):
                act.wait_ge(S["k_capped"], c + 1)
                nc.scalar.activation(ek[c % 2][:, :], ek[c % 2][:, :], ACT.Exp).then_inc(S["ek_ready"], 1)

            body(-1, False, True)
            with act.Fori(0, B - 1) as b:
                body(b, True, True)
            body(B - 1, True, False)

        @block.gpsimd
        def _(pool):
            def refine(i):
                pool.wait_ge(S["recip_done"], i + 1)
                pool.wait_ge(S["den_full"], i + 1)
                nc.gpsimd.tensor_tensor(fd[i % 2][:, :], bd[i % 2][:, :], bn[i % 2][:, :],
                                        ALU.mult).then_inc(S["newton"], 1)

            def weigh(c):
                pool.wait_ge(S["ek_ready"], c + 1)
                if c >= 2:
                    pool.wait_ge(S["num_scans"], 4 * (c - 1))
                nc.gpsimd.tensor_tensor(ekv[c % 2][:, :], ek[c % 2][:, :], kb[c % 2][:, :],
                                        ALU.mult).then_inc(S["ekv_ready"], 1)

            def body(b, G, R):
                hold(pool, "pool", go, b + 2)
                for j in range(FJ + 1):
                    c, layer = divmod(j, 2)
                    rec = R and j < HU
                    if R and 1 <= j <= HU:
                        refine(j - 1)
                    if G and j >= 1:
                        pool.wait_ge(S["h_hi"], j)
                        nc.gpsimd.tensor_tensor(hl[(j - 1) % 2][:, :], act_h[(j - 1) % 2][:, :],
                                                hh[(j - 1) % 2][:, :].bitcast(F32), ALU.subtract).then_inc(S["h_lo"], 1)
                    if rec:
                        if j == 0:
                            pool.wait_ge(S["k_in0"], 16)
                            weigh(0)
                        q = j % 2
                        pool.wait_ge(S["den_scans"], 2 * (j + 1))
                        nc.gpsimd.tensor_tensor(fd[q][:, 0:T - 1], fd[q][:, 0:T - 1], bd[q][:, 0:T - 1],
                                                ALU.add).then_inc(S["den_sum"], 1)
                        pool.wait_ge(S["num_scans"], 2 * (j + 1))
                        nc.gpsimd.tensor_tensor(fn[q][:, 0:T - 1], fn[q][:, 0:T - 1], bn[q][:, 0:T - 1],
                                                ALU.add).then_inc(S["num_sum"], 1)
                        if layer == 1 and c + 1 < CC:
                            weigh(c + 1)
                        pool.wait_ge(S["num_sum"], j + 1)
                        pool.wait_ge(S["lifted"], j + 1)
                        nc.gpsimd.tensor_tensor(fn[q][:, :], fn[q][:, :], eu[:, :], ALU.add).then_inc(S["num_full"], 1)
                    if R and j in (9, 10, 11):
                        for c1 in {9: (0,), 10: (1, 2), 11: (3,)}[j]:
                            pool.wait_ge(S["mixed"], c1 + 1)
                            pool.wait_ge(S[f"xb_in{c1 % 2}"], 16 * (c1 // 2 + 1))
                            nc.gpsimd.tensor_tensor(xs[c1 % 2][:, :], base0[:, c1, :], xs[c1 % 2][:, :],
                                                    ALU.add).then_inc(S["x1_ready"], 1)
                if R:
                    for c in range(CC):
                        pool.wait_ge(S["x_hi"], c + 1)
                        nc.gpsimd.tensor_tensor(xl[:, c, :], base1[:, c, :], xh[:, c, :].bitcast(F32),
                                                ALU.subtract).then_inc(S["x_lo"], 1)
                end_round(pool)

            body(-1, False, True)
            with pool.Fori(0, B - 1) as b:
                body(b, True, True)
            body(B - 1, True, False)

        @block.tensor
        def _(pe):
            def exact(ps, terms):
                ops = [(a, m) for (ah, al, mh, ml) in terms for (a, m) in ((ah, mh), (al, mh), (ah, ml))]
                for n, (a, m) in enumerate(ops):
                    ins = nc.tensor.matmul(ps, a, m, start=n == 0, stop=n == len(ops) - 1)
                return ins

            def down(j):
                pe.wait_ge(S["h_lo"], j + 1)
                K = P if j < FJ - 1 else FLAST
                for c in range(CC):
                    s = slice((2 * CC + c) * P, (2 * CC + c + 1) * P)
                    a = (wh[0:K, j, s], wl[0:K, j, s])
                    m = (hh[j % 2][0:K, :], hl[j % 2][0:K, :])
                    for n, (l, r) in enumerate(((a[0], m[0]), (a[1], m[0]), (a[0], m[1]))):
                        ins = nc.tensor.matmul(ps_d[c][:, :], l, r, start=(j == 0 and n == 0),
                                               stop=(j == FJ - 1 and n == 2))
                ins.then_inc(S["down_done"], 1)

            def mix(c):
                if c == 0:
                    pe.wait_ge(S["picked_t"], 1)
                else:
                    pe.wait_ge(S["mixed"], c)
                nc.tensor.matmul(ps_b[:, :], eb[:, c * P:(c + 1) * P], picked_t, start=True,
                                 stop=True).then_inc(S["mix_done"], 1)

            def body(b, G, R):
                hold(pe, "pe", go, b + 2)
                for j in range(FJ):
                    if R and j == 9:
                        pe.wait_ge(S["picked_t"], 1)
                        nc.tensor.matmul(ps_a[:, :], ones[0:E, :], picked_t, start=True,
                                         stop=True).then_inc(S["spread_done"], 1)
                        mix(0)
                    if R and j == 10:
                        mix(2)
                    if G:
                        if j >= 1:
                            pe.wait_ge(S["silu_done"], j)
                        exact(ps_g[:, :], [(wh[:, j, c * P:(c + 1) * P], wl[:, j, c * P:(c + 1) * P],
                                            xh[:, c, :], xl[:, c, :]) for c in range(CC)]).then_inc(S["gate_done"], 1)
                    if R and j == 9:
                        mix(1)
                    if R and j == 10:
                        mix(3)
                    if G:
                        if j >= 1:
                            pe.wait_ge(S["h_full"], j)
                        o = CC * P
                        exact(ps_u[:, :], [(wh[:, j, o + c * P:o + (c + 1) * P], wl[:, j, o + c * P:o + (c + 1) * P],
                                            xh[:, c, :], xl[:, c, :]) for c in range(CC)]).then_inc(S["up_done"], 1)
                    if R and j == 7:
                        pe.wait_ge(S["base0_ready"], CC)
                        for n in range(TT):
                            for c in range(CC):
                                ins = nc.tensor.matmul(ps_a[:, n * E:(n + 1) * E], base0[:, c, n * P:(n + 1) * P],
                                                       rw[:, c, :], start=c == 0, stop=c == CC - 1)
                        ins.then_inc(S["logits_done"], 1)
                    if R and j == 8:
                        pe.wait_ge(S["picked"], 1)
                        for n in range(TT):
                            ins = nc.tensor.transpose(ps_b[0:E, n * P:(n + 1) * P], picked[:, n, :], ident[:, :])
                        ins.then_inc(S["pick_done"], 1)
                    if G and j >= 1:
                        down(j - 1)
                if G:
                    down(FJ - 1)
                end_round(pe)

            body(-1, False, True)
            with pe.Fori(0, B - 1) as b:
                body(b, True, True)
            body(B - 1, True, False)

        @block.vector
        def _(dve):
            V = nc.vector

            def cap(c):
                dve.wait_ge(S[f"k_in{c % 2}"], 16 * (c // 2 + 1))
                if c >= 2:
                    dve.wait_ge(S["ekv_ready"], c - 1)
                V.tensor_scalar(ek[c % 2][:, :], kb[c % 2][:, :], KMAX, None, ALU.min).then_inc(S["k_capped"], 1)

            def scan_pair(src, fwd, bwd, d, done):
                V.tensor_tensor_scan(fwd[:, :], d.to_broadcast([P, T]), src[:, :], 0.0, ALU.mult,
                                     ALU.add).then_inc(done, 1)
                V.tensor_tensor_scan(bwd[:, T - 2::-1], src[:, T - 1:0:-1], d.to_broadcast([P, T - 1]), 0.0, ALU.add,
                                     ALU.mult).then_inc(done, 1)

            def finish(i):
                c, layer = divmod(i, 2)
                q = i % 2
                dve.wait_ge(S["recip_done"], i + 1)
                dve.wait_ge(S["num_full"], i + 1)
                V.scalar_tensor_tensor(out=fn[q][:, :], in0=fn[q][:, :], scalar=osc_cur[:, 0:1], in1=bn[q][:, :],
                                       op0=ALU.mult, op1=ALU.mult).then_inc(S["quotient"], 1)
                dve.wait_ge(S["quotient"], i + 1)
                dve.wait_ge(S["newton"], i + 1)
                dst = (base0, base1)[layer][:, c, :]
                V.scalar_tensor_tensor(out=dst, in0=fd[q][:, :], scalar=2.0, in1=fn[q][:, :], op0=ALU.subtract,
                                       op1=ALU.mult).then_inc(S["ratio_done"], 1)
                if layer == 0:
                    dve.wait_ge(S["ratio_done"], i + 1)
                    dve.wait_ge(S["t0_ready"], c + 1)
                    V.scalar_tensor_tensor(out=dst, in0=xs[c % 2][:, :], scalar=1.0, in1=dst, op0=ALU.add,
                                           op1=ALU.mult).then_inc(S["base0_ready"], 1)

            def body(b, G, R):
                hold(dve, "dve", go, b + 2)
                if R:
                    V.tensor_copy(dec_cur[:, :], dec[:, bass.ds(b + 1, 1), :].rearrange("p b n -> p (b n)")
                                  ).then_inc(S["cur_ready"], 1)
                    V.tensor_copy(osc_cur[:, :], osc[:, bass.ds(b + 1, 1)]).then_inc(S["cur_ready"], 1)
                    cap(0)
                    dve.wait_ge(S["cur_ready"], 2)
                for j in range(FJ + 1):
                    c, layer = divmod(j, 2)
                    q = j % 2
                    if G and j >= 1:
                        dve.wait_ge(S["silu_done"], j)
                        dve.wait_ge(S["up_done"], j)
                        V.tensor_tensor(act_h[(j - 1) % 2][:, :], act_h[(j - 1) % 2][:, :], ps_u[:, :],
                                        ALU.mult).then_inc(S["h_full"], 1)
                    if R and j < HU:
                        d = dec_cur[:, layer * CC + c:layer * CC + c + 1]
                        if G and j == 1:
                            hold(dve, "dve", y_out, 16 * CC * b)
                        dve.wait_ge(S["ek_ready"], c + 1)
                        scan_pair(ek[c % 2], fd[q], bd[q], d, S["den_scans"])
                        if j >= 1:
                            finish(j - 1)
                        dve.wait_ge(S["ekv_ready"], c + 1)
                        scan_pair(ekv[c % 2], fn[q], bn[q], d, S["num_scans"])
                        dve.wait_ge(S["den_sum"], j + 1)
                        dve.wait_ge(S["e_ready"], j + 1)
                        V.scalar_tensor_tensor(out=bd[q][:, :], in0=eu[:, :], scalar=EXP_KMAX, in1=fd[q][:, :],
                                               op0=ALU.min, op1=ALU.add).then_inc(S["den_full"], 1)
                        V.scalar_tensor_tensor(out=eu[:, :], in0=eu[:, :], scalar=EXP_KMAX, in1=kb[c % 2][:, :],
                                               op0=ALU.min, op1=ALU.mult).then_inc(S["lifted"], 1)
                        dve.wait_ge(S["den_full"], j + 1)
                        V.tensor_scalar(bd[q][:, :], bd[q][:, :], DEN_MIN, None, ALU.max).then_inc(S["den_ready"], 1)
                        if layer == 0 and c + 1 < CC:
                            cap(c + 1)
                    if R and j == HU:
                        finish(HU - 1)
                        top_k()
                    if R and j in (9, 10, 11):
                        for c1 in {9: (0, 1), 10: (2,), 11: (3,)}[j]:
                            mixture(c1)
                        for c1 in {9: (), 10: (0,), 11: (1, 2, 3)}[j]:
                            dve.wait_ge(S["t1_ready"], c1 + 1)
                            dve.wait_ge(S["ratio_done"], HU)
                            V.scalar_tensor_tensor(out=base1[:, c1, :], in0=base0[:, c1, :], scalar=1.0,
                                                   in1=base1[:, c1, :], op0=ALU.add,
                                                   op1=ALU.mult).then_inc(S["base1_ready"], 1)
                if G:
                    dve.wait_ge(S["down_done"], FJ)
                    dve.wait_ge(S["x1_back"], 16 * CC)
                    for c in range(CC):
                        V.tensor_tensor(x1b[c][:, :], x1b[c][:, :], ps_d[c][:, :], ALU.add).then_inc(S["down_used"], 1)
                end_round(dve)

            def top_k():
                chain = [0]

                def link(ins):
                    chain[0] += 1
                    ins.then_inc(S["l0_chain"], 1)

                def linked():
                    dve.wait_ge(S["l0_chain"], chain[0])

                dve.wait_ge(S["logits_done"], 1)
                dve.wait_ge(S["ratio_done"], HU)
                link(V.tensor_tensor(logits, ps_a[:, 0:TT * E].rearrange("p (t e) -> p t e", e=E),
                                     rb[:, None, :].to_broadcast([P, TT, E]), ALU.add))
                linked()
                for n in range(TT):
                    link(V.max(top8[:, n, :], logits[:, n, :]))
                linked()
                V.tensor_scalar(neg_max[:, :], top8[:, :, 0], -1.0, None, ALU.mult).then_inc(S["top_done"], 1)
                for n in range(TT):
                    link(V.match_replace(marked[:, n, :], top8[:, n, :], logits[:, n, :], TAKEN))
                linked()
                link(V.tensor_tensor(marked, marked, logits, ALU.not_equal))
                dve.wait_ge(S["exps_done"], 1)
                link(V.reciprocal(zinv[:, :], zsum[:, :]))
                linked()
                link(V.tensor_tensor(picked, marked, exps, ALU.mult))
                linked()
                V.tensor_tensor(picked, picked, zinv[:, :, None].to_broadcast([P, TT, E]),
                                ALU.mult).then_inc(S["picked"], 1)

            def mixture(c):
                if c == 0:
                    dve.wait_ge(S["spread_done"], 1)
                V.tensor_tensor(base0[:, c, :], base0[:, c, :], ps_a[:, :], ALU.mult).then_inc(S["mix_half"], 1)
                dve.wait_ge(S["mix_half"], c + 1)
                dve.wait_ge(S["mix_done"], c + 1)
                V.tensor_tensor(base0[:, c, :], base0[:, c, :], ps_b[:, :], ALU.add).then_inc(S["mixed"], 1)

            body(-1, False, True)
            with dve.Fori(0, B - 1) as b:
                body(b, True, True)
            body(B - 1, True, False)


def kernel(**inputs):
    import numpy as np
    import concourse.bacc as bacc
    from concourse.bass_utils import run_bass_kernel_spmd

    a = {n: np.asarray(v) for n, v in inputs.items()}

    def columns(v):
        return v.reshape(CC, P).T

    def chunked(idx):
        idx = np.pad(idx, ((0, FJ * P - F), (0, 0)))
        return idx.reshape(FJ, P, CC, P).transpose(0, 3, 2, 1).reshape(FJ, P, CC * P)

    down = np.pad(a["L1_ffn_down_idx"], ((0, 0), (0, FJ * P - F))).T.reshape(FJ, P, C)
    idx = np.concatenate([chunked(a["L1_ffn_gate_idx"]), chunked(a["L1_ffn_up_idx"]), down], axis=2)
    idx = idx.reshape(FJ, P, WJ // SB, SB).transpose(0, 2, 1, 3).reshape(NS, P, SB)
    arrays = {
        "x": a["x"].transpose(0, 2, 1).reshape(B, CC, P, T),
        "k": a["fside_BxSxS_0"].transpose(0, 2, 1).reshape(B, CC, P, T),
        "cond": a["cond_512"].T,
        "w": np.concatenate([columns(a["L0_cond_w"]), columns(a["L1_cond_w"])], axis=1),
        "u": np.concatenate([columns(a["L0_cond_u"]), columns(a["L1_cond_u"])], axis=1),
        "router_w": a["L0_ffn_router_weight"].T.reshape(CC, P, E).transpose(1, 0, 2),
        "router_b": a["L0_ffn_router_bias"].reshape(1, E),
        "expert_b": a["L0_ffn_expert_bias"],
        "lut": a["L1_ffn_lut"].reshape(1, 16),
        "idx": idx,
    }
    arrays = {n: np.ascontiguousarray(v) for n, v in arrays.items()}
    nc = bacc.Bacc("TRN2", target_bir_lowering=False, num_devices=1, dynamic_dma_scratch_size=1024)
    aps = {n: nc.dram_tensor(f"in_{n}", v.shape, mybir.dt.from_np(v.dtype), kind="ExternalInput").ap()
           for n, v in arrays.items()}
    y = nc.dram_tensor("y", (B, CC, P, T), F32, kind="ExternalOutput").ap()
    build(nc, y=y, **aps)
    r = run_bass_kernel_spmd(nc, [{f"in_{n}": v for n, v in arrays.items()}], core_ids=[0])
    out = r.results[0]["y"]
    return np.ascontiguousarray(out.reshape(B, C, T).transpose(0, 2, 1))
```

```python
from contextlib import ExitStack

import concourse.bass as bass
from concourse import mybir

F32 = mybir.dt.float32
F32R = mybir.dt.float32r
I32 = mybir.dt.int32
I16 = mybir.dt.int16
U8 = mybir.dt.uint8
ALU = mybir.AluOpType
ACT = mybir.ActivationFunctionType

P = 128
B, T, C = 4, 512, 512
CC = C // P
E = 64
TT = T // P
F = 1376
FJ = -(-F // P)
FLAST = F - (FJ - 1) * P
WJ = 3 * CC * P
SB = CC * P
NS = FJ * WJ // SB
HU = 2 * CC
KMAX = 30.0
EXP_KMAX = 1.0686474581524463e13
DEN_MIN = 1e-8
BIT0 = 0x20
TAKEN = -3.0e38


def build(nc, x, k, cond, w, u, router_w, router_b, expert_b, lut, idx, y):
    ctx = ExitStack()
    with ctx:
        def sb(name, shape, dt=F32, into=ctx):
            return into.enter_context(nc.sbuf_tensor(name, shape, dt))

        def ps(name):
            return ctx.enter_context(nc.psum_tensor(name, [P, T], F32))

        def sem(name):
            return ctx.enter_context(nc.semaphore(name))

        x1_dram = nc.dram_tensor("x1_scratch", (B, CC, P, T), F32, kind="Internal").ap()

        xh = sb("xh", [P, CC, T], F32R)
        xl = sb("xl", [P, CC, T], F32R)
        base1 = sb("base1", [P, CC, T])
        act_h = [sb(f"act_h{p}", [P, T]) for p in range(2)]
        hh = [sb(f"hh{p}", [P, T], F32R) for p in range(2)]
        hl = [sb(f"hl{p}", [P, T], F32R) for p in range(2)]
        rw = sb("rw", [P, CC, E])
        rb = sb("rb", [P, E])
        eb = sb("eb", [E, C])
        ones = sb("ones", [P, P])
        ident = sb("ident", [P, P])
        cond_t = sb("cond_t", [P, B])
        w_in = sb("w_in", [P, 2 * CC])
        u_in = sb("u_in", [P, 2 * CC])
        tf = sb("tf", [P, 4, B])
        dec0 = sb("dec0", [P, 2, 2 * CC])
        dec = sb("dec", [P, B, 2 * CC])
        osc = sb("osc", [P, B])
        osc2 = sb("osc2", [P, B])
        dec_cur = sb("dec_cur", [P, 2 * CC])
        osc_cur = sb("osc_cur", [P, 1])
        kb = [sb(f"kb{p}", [P, T]) for p in range(2)]
        idx_sb = [sb(f"idx_sb{p}", [P, SB], I32) for p in range(2)]
        idx16 = [sb(f"idx16_{p}", [P, SB], I16) for p in range(2)]
        bits03 = [sb(f"bits03_{p}", [P, SB], I16) for p in range(2)]
        lut_in = sb("lut_in", [P, 16])
        lut_d = sb("lut_d", [P, 8])
        ps_g, ps_u, ps_a, ps_b = ps("ps_g"), ps("ps_u"), ps("ps_a"), ps("ps_b")
        ps_d = [ps(f"ps_d{c}") for c in range(CC)]

        consts_in = sem("consts_in")
        late_consts_in = sem("late_consts_in")
        pool_consts = sem("pool_consts")
        cond_sum = sem("cond_sum")
        setup_exp = sem("setup_exp")
        setup_dve = sem("setup_dve")
        lut_diff = sem("lut_diff")
        round_done = sem("round_done")
        go = sem("go")
        held = {n: sem(f"held_{n}") for n in ("act", "dve", "pool", "pe", "sp")}
        idx_in = [sem("idx_in0"), sem("idx_in1")]
        idx_narrow = sem("idx_narrow")
        bits03_ready = sem("bits03_ready")
        bits12_ready = sem("bits12_ready")
        leaves_act = sem("leaves_act")
        leaves_pool = sem("leaves_pool")
        pairs_done = sem("pairs_done")
        fours_done = sem("fours_done")
        weight_full = sem("weight_full")
        weight_hi = sem("weight_hi")
        weight_lo = sem("weight_lo")
        y_out = sem("y_out")
        names = """k_ahead k_in0 k_in1 x_in0 x_in1 x_in2 x_in3 xb_in0 xb_in1 x1_out0 x1_out1 x1_back cur_ready k_capped ek_ready ekv_ready
            e_ready e_capped t0_ready den_scans den_part num_scans num_half den_sum num_sum den_ready lifted num_full ln_done
            recip_done newton quotient ratio_done base0_ready logits_done l0_chain top_done exps_done picked picked_t
            pick_done spread_done mix_done mix_half mixed x1_ready t1_ready base1_ready x_hi x_lo gate_done up_done
            silu_done h_full h_hi h_lo down_done bank_done down_used""".split()
        S = {n: sem(n) for n in names}
        nums = sorted(s.num for s in S.values())
        assert nums == list(range(nums[0], nums[0] + len(nums)))
        cleared = range(nums[0], nums[-1] + 1)

        def hold(eng, name, s, value):
            eng.wait_ge(s, value)
            eng.sem_inc(held[name], 1)

        def begin_round(eng, name, n):
            if not isinstance(n, int) or n > 0:
                hold(eng, name, go, n)

        def end_round(eng):
            eng.drain().then_inc(round_done, 1)

        def next_round(sp):
            sp.wait_ge(round_done, 4)
            sp.sem_clear(cleared)
            sp.sem_clear(round_done)
            sp.sem_inc(go, 1)

        k_first = [[sem(f"k_first{r}{c}") for c in range(CC)] for r in range(2)]
        x1_first = [sem(f"x1_first{c}") for c in range(CC)]
        x_first = [[sem(f"x_first{r}{c}") for c in range(CC)] for r in range(2)]

        v = dict(locals())
        block_first(nc, v)
        v["wh"] = sb("wh", [P, FJ, WJ], F32R)
        v["wl"] = sb("wl", [P, FJ, WJ], F32R)
        block_lookup(nc, v)
        block_rounds(nc, v, [("loop", 2, B - 2), (B, B - 1, None)])


def row(a, b, c):
    return a.rearrange("b c p t -> (b c p) t")[bass.ds((b * CC + c) * P, P), :]


class Products:

    def __init__(self, nc, v):
        self.nc, self.S = nc, v["S"]
        self.v = v

    def exact(self, out, terms):
        ops = [(a, m) for (ah, al, mh, ml) in terms for (a, m) in ((ah, mh), (al, mh), (ah, ml))]
        for n, (a, m) in enumerate(ops):
            ins = self.nc.tensor.matmul(out, a, m, start=n == 0, stop=n == len(ops) - 1)
        return ins

    def into_hidden(self, j, off, out):
        wh, wl, xh, xl = (self.v[n] for n in ("wh", "wl", "xh", "xl"))
        return self.exact(out, [(wh[:, j, off + c * P:off + (c + 1) * P], wl[:, j, off + c * P:off + (c + 1) * P],
                                 xh[:, c, :], xl[:, c, :]) for c in range(CC)])

    def gate(self, pe, j):
        if j >= 1:
            pe.wait_ge(self.S["silu_done"], j)
        self.into_hidden(j, 0, self.v["ps_g"][:, :]).then_inc(self.S["gate_done"], 1)

    def up(self, pe, j):
        if j >= 1:
            pe.wait_ge(self.S["h_full"], j)
        self.into_hidden(j, CC * P, self.v["ps_u"][:, :]).then_inc(self.S["up_done"], 1)

    def down(self, pe, j):
        wh, wl, hh, hl, ps_d = (self.v[n] for n in ("wh", "wl", "hh", "hl", "ps_d"))
        pe.wait_ge(self.S["h_lo"], j + 1)
        K = P if j < FJ - 1 else FLAST
        for c in range(CC):
            s = slice((2 * CC + c) * P, (2 * CC + c + 1) * P)
            for n, (a, m) in enumerate(((wh, hh), (wl, hh), (wh, hl))):
                ins = self.nc.tensor.matmul(ps_d[c][:, :], a[0:K, j, s], m[j % 2][0:K, :],
                                            start=(j == 0 and n == 0), stop=(j == FJ - 1 and n == 2))
            if j == FJ - 1:
                ins.then_inc(self.S["bank_done"], 1)
        if j < FJ - 1:
            ins.then_inc(self.S["down_done"], 1)

    def silu(self, wait, j, q, reused):
        wait(self.S["gate_done"], j + 1)
        if reused:
            wait(self.S["h_lo"], j - 1)
        self.nc.scalar.activation(self.v["act_h"][q][:, :], self.v["ps_g"][:, :],
                                  ACT.Silu).then_inc(self.S["silu_done"], 1)

    def hidden(self, wait, j, q):
        wait(self.S["silu_done"], j + 1)
        wait(self.S["up_done"], j + 1)
        h = self.v["act_h"][q][:, :]
        self.nc.vector.tensor_tensor(h, h, self.v["ps_u"][:, :], ALU.mult).then_inc(self.S["h_full"], 1)

    def split_hi(self, wait, j, q, reused):
        wait(self.S["h_full"], j + 1)
        if reused:
            wait(self.S["down_done"], j - 1)
        self.nc.scalar.activation(self.v["hh"][q][:, :], self.v["act_h"][q][:, :],
                                  ACT.Copy).then_inc(self.S["h_hi"], 1)

    def split_lo(self, wait, j, q):
        wait(self.S["h_hi"], j + 1)
        self.nc.gpsimd.tensor_tensor(self.v["hl"][q][:, :], self.v["act_h"][q][:, :],
                                     self.v["hh"][q][:, :].bitcast(F32), ALU.subtract).then_inc(self.S["h_lo"], 1)

    def fetch_x1(self, sp, b, x1b):
        for c in range(CC):
            sp.dma_start(x1b[c][:, :], row(self.v["x1_dram"], b, c)).then_inc(self.S["x1_back"], 16)

    def store_y(self, sp, b, x1b):
        for c in range(CC):
            sp.wait_ge(self.S["down_used"], c + 1)
            sp.dma_start(row(self.v["y"], b, c), x1b[c][:, :]).then_inc(self.v["y_out"], 16)

    def add_x1(self, dve, x1b):
        dve.wait_ge(self.S["x1_back"], 16 * CC)
        for c in range(CC):
            dve.wait_ge(self.S["bank_done"], c + 1)
            self.nc.vector.tensor_tensor(x1b[c][:, :], x1b[c][:, :], self.v["ps_d"][c][:, :],
                                         ALU.add).then_inc(self.S["down_used"], 1)

    def input_hi(self, act, after_products, fresh):
        if after_products:
            act.wait_ge(self.S["up_done"], FJ)
        for c in range(CC):
            if fresh:
                act.wait_ge(self.S["base1_ready"], c + 1)
            self.nc.scalar.activation(self.v["xh"][:, c, :], self.v["base1"][:, c, :],
                                      ACT.Copy).then_inc(self.S["x_hi"], 1)

    def input_lo(self, eng, of, chunks):
        for c in chunks:
            eng.wait_ge(self.S["x_hi"], c + 1)
            of.tensor_tensor(self.v["xl"][:, c, :], self.v["base1"][:, c, :], self.v["xh"][:, c, :].bitcast(F32),
                             ALU.subtract).then_inc(self.S["x_lo"], 1)


def block_first(nc, v):
    sb, S, begin_round, end_round, next_round = (v[n] for n in "sb S begin_round end_round next_round".split())
    (x, k, x1_dram, rw, rb, eb, ones, ident, u_in, dec, osc2, base1, xh, xl) = (
        v[n] for n in "x k x1_dram rw rb eb ones ident u_in dec osc2 base1 xh xl".split())
    ps_a, ps_b, k_first, x_first = (v[n] for n in "ps_a ps_b k_first x_first".split())
    ps_den, ps_num, ps_mix = [v["ps_g"], v["ps_u"]], v["ps_d"][0:2], v["ps_d"][2:4]
    R2 = 2
    U = R2 * HU
    NQ = 4

    def unit(u):
        r, i = divmod(u, HU)
        return r, i, i % CC, i // CC

    def chunk_at(u):
        if u < U and unit(u)[3] == 0:
            return unit(u)[0], unit(u)[2]

    MIXED = {1: (0,), 2: (1,), 3: (2,), 4: (3,)}
    BASE1 = {5: (0, 1), 6: (2, 3)}
    HIGH = {6: (0, 1), 7: (2, 3)}
    LOW = {7: (0, 1), 8: (2, 3)}

    def tail(table, u, behind=0):
        return [(r, c) for r in range(R2) for c in table.get(u - HU * (r + 1) + 1 - behind, ())]

    with ExitStack() as tmp:
        def t(name, shape, dt=F32):
            return sb(f"{name}_first", shape, dt, tmp)

        kb = [[t(f"kb{r}{c}", [P, T]) for c in range(CC)] for r in range(R2)]
        xb = [[t(f"xb{r}{c}", [P, T]) for c in range(CC)] for r in range(R2)]
        base0 = [t(f"base0{r}", [P, CC, T]) for r in range(R2)]
        base1_of = [t("base1", [P, CC, T]), base1]
        ek = [t(f"ek{c}", [P, T]) for c in range(CC)]
        ekv = [t(f"ekv{c}", [P, T]) for c in range(CC)]
        x1s = [t(f"x1s{c}", [P, T]) for c in range(CC)]
        eu, ev, fd, bd, fn, bn, den, rec, dr, quo = ([t(f"{n}{q}", [P, T]) for q in range(NQ)] for n in
                                                     "eu ev fd bd fn bn den rec dr quo".split())
        logits, marked, exps, picked = (t(n, [P, TT, E]) for n in "logits marked exps picked".split())
        picked_t = t("picked_t", [E, T])
        top8 = t("top8", [P, TT, 8])
        neg_max = t("neg_max", [P, TT])
        zsum = t("zsum", [P, TT])
        zinv = t("zinv", [P, TT])
        block = tmp.enter_context(nc.Block())

        @block.sync
        def _(sp):
            def load(a, dst, sems, r, c):
                sp.dma_start(dst[r][c][:, :], row(a, r, c)).then_inc(sems[r][c], 16)

            load(k, kb, k_first, 0, 0)
            load_constants(nc, v, sp, late=False)
            load(x, xb, x_first, 0, 0)
            for c in range(1, CC):
                load(k, kb, k_first, 0, c)
                load(x, xb, x_first, 0, c)
            load_constants(nc, v, sp, late=True)
            for c in range(CC):
                load(k, kb, k_first, 1, c)
                load(x, xb, x_first, 1, c)
            for s in range(2):
                sp.dma_start(v["idx_sb"][s][:, :], v["idx"][s]).then_inc(v["idx_in"][s], 16)
            for n in range(R2 * CC):
                r, c = divmod(n, CC)
                sp.wait_ge(S["x1_ready"], n + 1)
                sp.dma_start(row(x1_dram, r, c), x1s[c][:, :]).then_inc(v["x1_first"][c], 16)
            for c in range(CC):
                sp.wait_ge(v["x1_first"][c], 16 * R2)
            next_round(sp)

        @block.scalar
        def _(act):
            def ek_of(r, c):
                act.wait_ge(S["k_capped"], r * CC + c + 1)
                nc.scalar.activation(ek[c][:, :], ek[c][:, :], ACT.Exp).then_inc(S["ek_ready"], 1)

            def eu_of(u):
                r, i, c, layer = unit(u)
                act.wait_ge(k_first[r][c], 16)
                if u >= NQ:
                    act.wait_ge(S["den_sum"], u - NQ + 1)
                    act.wait_ge(S["lifted"], u - NQ + 1)
                n = layer * CC + c
                nc.scalar.activation(eu[u % NQ][:, :], kb[r][c][:, :], ACT.Exp,
                                     bias=u_in[:, n:n + 1]).then_inc(S["e_ready"], 1)

            def sigmoid_x(r):
                for c in range(CC):
                    act.wait_ge(x_first[r][c], 16)
                    nc.scalar.activation(base0[r][:, c, :], xb[r][c][:, :], ACT.Sigmoid).then_inc(S["t0_ready"], 1)

            def sigmoid_x1(r, c):
                act.wait_ge(S["x1_ready"], r * CC + c + 1)
                nc.scalar.activation(base0[r][:, c, :], x1s[c][:, :], ACT.Sigmoid).then_inc(S["t1_ready"], 1)

            constants_act(nc, v, act)
            ek_of(0, 0)
            eu_of(0)
            ek_of(0, 1)
            sigmoid_x(0)
            nc.scalar.preload_act_table_set("natural_log_exp_and_others")
            for u in range(U):
                r, i, c, layer = unit(u)
                q = u % NQ
                if u + 1 < U:
                    eu_of(u + 1)
                if chunk_at(u + 2):
                    ek_of(*chunk_at(u + 2))
                for r1, c1 in tail(HIGH, u):
                    if r1 == 0:
                        act.wait_ge(S["base1_ready"], c1 + 1)
                        nc.scalar.activation(xh[:, c1, :], base1_of[0][:, c1, :], ACT.Copy).then_inc(S["x_hi"], 1)
                if i == 6:
                    act.wait_ge(S["top_done"], r + 1)
                    for n in range(TT):
                        ins = nc.scalar.activation(exps[:, n, :], logits[:, n, :], ACT.Exp,
                                                   bias=neg_max[:, n:n + 1], accum_out=zsum[:, n:n + 1])
                    ins.then_inc(S["exps_done"], 1)
                if i == 7:
                    act.wait_ge(S["pick_done"], r + 1)
                    nc.scalar.activation(picked_t[:, :], ps_b[0:E, :], ACT.Copy).then_inc(S["picked_t"], 1)
                act.wait_ge(S["den_ready"], u + 1)
                if u >= NQ:
                    act.wait_ge(S["newton"], u - NQ + 1)
                    act.wait_ge(S["quotient"], u - NQ + 1)
                nc.scalar.activation(rec[q][:, :], den[q][:, :], ACT.Ln).then_inc(S["ln_done"], 1)
                act.wait_ge(S["ln_done"], u + 1)
                nc.scalar.activation(rec[q][:, :], rec[q][:, :], ACT.Exp, scale=-1.0).then_inc(S["recip_done"], 1)
                if i == 5 and r + 1 < R2:
                    sigmoid_x(r + 1)
                    nc.scalar.preload_act_table_set("natural_log_exp_and_others")
                if u == HU + 3:
                    for c1 in range(CC):
                        sigmoid_x1(0, c1)
                    nc.scalar.preload_act_table_set("natural_log_exp_and_others")
            for s in range(2):
                act.wait_ge(v["idx_in"][s], 16)
                narrow_idx(nc, v, s)
            for c1 in range(CC):
                sigmoid_x1(R2 - 1, c1)
            end_round(act)

        @block.gpsimd
        def _(pool):
            def refine(u):
                q = u % NQ
                pool.wait_ge(S["recip_done"], u + 1)
                if u >= NQ:
                    pool.wait_ge(S["ratio_done"], u - NQ + 1)
                nc.gpsimd.tensor_tensor(dr[q][:, :], den[q][:, :], rec[q][:, :], ALU.mult).then_inc(S["newton"], 1)

            def weigh(r, c):
                pool.wait_ge(k_first[r][c], 16)
                pool.wait_ge(S["ek_ready"], r * CC + c + 1)
                if r >= 1:
                    pool.wait_ge(S["num_scans"], 2 * (HU * (r - 1) + CC + c + 1))
                nc.gpsimd.tensor_tensor(ekv[c][:, :], ek[c][:, :], kb[r][c][:, :], ALU.mult).then_inc(S["ekv_ready"], 1)

            def gate_base0(u):
                r, i, c, layer = unit(u)
                if layer == 0:
                    pool.wait_ge(S["ratio_done"], u + 1)
                    pool.wait_ge(S["t0_ready"], r * CC + c + 1)
                    nc.gpsimd.tensor_tensor(base0[r][:, c, :], base0[r][:, c, :], quo[u % NQ][:, :],
                                            ALU.mult).then_inc(S["base0_ready"], 1)

            constants_pool(nc, v, pool)
            weigh(0, 0)
            for u in range(U):
                r, i, c, layer = unit(u)
                q = u % NQ
                if u >= 1:
                    refine(u - 1)
                pool.wait_ge(S["e_capped"], u + 1)
                if u >= NQ:
                    pool.wait_ge(S["num_sum"], u - NQ + 1)
                nc.gpsimd.tensor_tensor(ev[q][:, :], eu[q][:, :], kb[r][c][:, :], ALU.mult).then_inc(S["lifted"], 1)
                if layer == 1:
                    pool.wait_ge(S["num_scans"], 2 * (u + 1))
                    nc.gpsimd.tensor_tensor(fn[q][:, 0:T - 1], fn[q][:, 0:T - 1], bn[q][:, 0:T - 1],
                                            ALU.add).then_inc(S["num_half"], 1)
                if chunk_at(u + 1):
                    weigh(*chunk_at(u + 1))
                if u >= 1:
                    gate_base0(u - 1)
                for r1, c1 in tail(LOW, u):
                    if r1 == 0:
                        pool.wait_ge(S["x_hi"], c1 + 1)
                        nc.gpsimd.tensor_tensor(xl[:, c1, :], base1_of[0][:, c1, :], xh[:, c1, :].bitcast(F32),
                                                ALU.subtract).then_inc(S["x_lo"], 1)
            refine(U - 1)
            end_round(pool)

        @block.tensor
        def _(pe):
            def add(out, m, n, first, last):
                return nc.tensor.matmul(out[:, 0:n], ident[:, :], m[:, 0:n], start=first, stop=last)

            def total_den(u):
                q, out = u % NQ, ps_den[u % 2]
                pe.wait_ge(S["den_scans"], 2 * u + 2)
                if u >= 2:
                    pe.wait_ge(S["den_ready"], u - 1)
                add(out, fd[q], T, True, False)
                add(out, bd[q], T - 1, False, False)
                pe.wait_ge(S["e_capped"], u + 1)
                add(out, eu[q], T, False, True).then_inc(S["den_sum"], 1)

            def total_num(u):
                r, i, c, layer = unit(u)
                q, out = u % NQ, ps_num[u % 2]
                if layer == 0:
                    pe.wait_ge(S["num_scans"], 2 * u + 2)
                else:
                    pe.wait_ge(S["num_half"], r * CC + c + 1)
                if u >= 2:
                    pe.wait_ge(S["quotient"], u - 1)
                add(out, fn[q], T, True, False)
                if layer == 0:
                    add(out, bn[q], T - 1, False, False)
                pe.wait_ge(S["lifted"], u + 1)
                add(out, ev[q], T, False, True).then_inc(S["num_sum"], 1)

            def mix(r, c):
                n = r * CC + c
                if c == 0:
                    pe.wait_ge(S["picked_t"], r + 1)
                    nc.tensor.matmul(ps_a[:, :], ones[0:E, :], picked_t[:, :], start=True,
                                     stop=True).then_inc(S["spread_done"], 1)
                if n >= 2:
                    pe.wait_ge(S["x1_ready"], n - 1)
                add(ps_mix[c % 2], xb[r][c], T, True, False)
                nc.tensor.matmul(ps_mix[c % 2][:, :], eb[:, c * P:(c + 1) * P], picked_t[:, :], start=False,
                                 stop=True).then_inc(S["mix_done"], 1)

            constants_pe(nc, v, pe)
            for u in range(U):
                r, i, c, layer = unit(u)
                if i == 7:
                    pe.wait_ge(S["picked"], r + 1)
                    for n in range(TT):
                        ins = nc.tensor.transpose(ps_b[0:E, n * P:(n + 1) * P], picked[:, n, :], ident[:, :])
                    ins.then_inc(S["pick_done"], 1)
                total_den(u)
                if i == 5:
                    pe.wait_ge(v["late_consts_in"], 64)
                    pe.wait_ge(S["base0_ready"], (r + 1) * CC)
                    for n in range(TT):
                        for c1 in range(CC):
                            ins = nc.tensor.matmul(ps_a[:, n * E:(n + 1) * E], base0[r][:, c1, n * P:(n + 1) * P],
                                                   rw[:, c1, :], start=c1 == 0, stop=c1 == CC - 1)
                    ins.then_inc(S["logits_done"], 1)
                total_num(u)
                for r1, c1 in tail(MIXED, u, -1):
                    mix(r1, c1)
            for n in range(1, CC):
                for r1, c1 in tail(MIXED, U - 1 + n, -1):
                    mix(r1, c1)
            end_round(pe)

        @block.vector
        def _(dve):
            V = nc.vector

            def cap(r, c):
                dve.wait_ge(k_first[r][c], 16)
                if r >= 1:
                    dve.wait_ge(S["den_scans"], 2 * (HU * (r - 1) + CC + c + 1))
                    dve.wait_ge(S["ekv_ready"], CC * (r - 1) + c + 1)
                V.tensor_scalar(ek[c][:, :], kb[r][c][:, :], KMAX, None, ALU.min).then_inc(S["k_capped"], 1)

            def scan_pair(src, fwd, bwd, d, done):
                V.tensor_tensor_scan(fwd[:, :], d.to_broadcast([P, T]), src[:, :], 0.0, ALU.mult,
                                     ALU.add).then_inc(done, 1)
                V.tensor_tensor_scan(bwd[:, T - 2::-1], src[:, T - 1:0:-1], d.to_broadcast([P, T - 1]), 0.0, ALU.add,
                                     ALU.mult).then_inc(done, 1)

            def finish(u):
                r, i, c, layer = unit(u)
                q = u % NQ
                dve.wait_ge(S["num_sum"], u + 1)
                dve.wait_ge(S["recip_done"], u + 1)
                if u >= NQ and unit(u - NQ)[3] == 0:
                    dve.wait_ge(S["base0_ready"], unit(u - NQ)[0] * CC + unit(u - NQ)[2] + 1)
                V.scalar_tensor_tensor(out=quo[q][:, :], in0=ps_num[u % 2][:, :], scalar=osc2[:, r:r + 1],
                                       in1=rec[q][:, :], op0=ALU.mult, op1=ALU.mult).then_inc(S["quotient"], 1)
                dve.wait_ge(S["quotient"], u + 1)
                dve.wait_ge(S["newton"], u + 1)
                dst = (quo[q][:, :], base1_of[r][:, c, :])[layer]
                V.scalar_tensor_tensor(out=dst, in0=dr[q][:, :], scalar=2.0, in1=quo[q][:, :], op0=ALU.subtract,
                                       op1=ALU.mult).then_inc(S["ratio_done"], 1)

            def mixture(r, c):
                n = r * CC + c
                dve.wait_ge(S["spread_done"], r + 1)
                V.tensor_tensor(base0[r][:, c, :], base0[r][:, c, :], ps_a[:, :], ALU.mult).then_inc(S["mix_half"], 1)
                dve.wait_ge(S["mix_half"], n + 1)
                dve.wait_ge(S["mix_done"], n + 1)
                if r >= 1:
                    dve.wait_ge(v["x1_first"][c], 16 * r)
                V.tensor_tensor(x1s[c][:, :], base0[r][:, c, :], ps_mix[c % 2][:, :], ALU.add).then_inc(S["x1_ready"], 1)

            def gate_base1(r, c):
                dve.wait_ge(S["t1_ready"], r * CC + c + 1)
                dve.wait_ge(S["ratio_done"], (r + 1) * HU)
                V.tensor_tensor(base1_of[r][:, c, :], base0[r][:, c, :], base1_of[r][:, c, :],
                                ALU.mult).then_inc(S["base1_ready"], 1)

            chain = [0]

            def link(ins):
                chain[0] += 1
                ins.then_inc(S["l0_chain"], 1)

            def linked():
                dve.wait_ge(S["l0_chain"], chain[0])

            def find_top():
                dve.wait_ge(S["logits_done"], r + 1)
                dve.wait_ge(v["late_consts_in"], 64)
                link(V.tensor_tensor(logits[:, :, :], ps_a[:, 0:TT * E].rearrange("p (t e) -> p t e", e=E),
                                     rb[:, None, :].to_broadcast([P, TT, E]), ALU.add))
                linked()
                for n in range(TT):
                    link(V.max(top8[:, n, :], logits[:, n, :]))
                linked()
                V.tensor_scalar(neg_max[:, :], top8[:, :, 0], -1.0, None, ALU.mult).then_inc(S["top_done"], 1)
                for n in range(TT):
                    link(V.match_replace(marked[:, n, :], top8[:, n, :], logits[:, n, :], TAKEN))
                linked()
                link(V.tensor_tensor(marked[:, :, :], marked[:, :, :], logits[:, :, :], ALU.not_equal))

            def weigh_top():
                dve.wait_ge(S["exps_done"], r + 1)
                link(V.reciprocal(zinv[:, :], zsum[:, :]))
                linked()
                link(V.tensor_tensor(picked[:, :, :], marked[:, :, :], exps[:, :, :], ALU.mult))
                linked()
                V.tensor_tensor(picked[:, :, :], picked[:, :, :], zinv[:, :, None].to_broadcast([P, TT, E]),
                                ALU.mult).then_inc(S["picked"], 1)

            cap(0, 0)
            cap(0, 1)
            constants_dve(nc, v, dve, late=False)
            for u in range(U):
                r, i, c, layer = unit(u)
                q = u % NQ
                d = dec[:, r, layer * CC + c:layer * CC + c + 1]
                dve.wait_ge(S["ek_ready"], r * CC + c + 1)
                if u >= NQ:
                    dve.wait_ge(S["den_sum"], u - NQ + 1)
                scan_pair(ek[c], fd[q], bd[q], d, S["den_scans"])
                dve.wait_ge(S["e_ready"], u + 1)
                V.tensor_scalar(eu[q][:, :], eu[q][:, :], EXP_KMAX, None, ALU.min).then_inc(S["e_capped"], 1)
                dve.wait_ge(S["ekv_ready"], r * CC + c + 1)
                if u >= NQ:
                    dve.wait_ge(S["num_sum"], u - NQ + 1)
                scan_pair(ekv[c], fn[q], bn[q], d, S["num_scans"])
                if u == 0:
                    constants_dve(nc, v, dve, late=True)
                if i == 6:
                    find_top()
                if chunk_at(u + 2):
                    cap(*chunk_at(u + 2))
                if u >= 1:
                    finish(u - 1)
                dve.wait_ge(S["den_sum"], u + 1)
                if u >= NQ:
                    dve.wait_ge(S["newton"], u - NQ + 1)
                V.tensor_scalar(den[q][:, :], ps_den[u % 2][:, :], DEN_MIN, None, ALU.max).then_inc(S["den_ready"], 1)
                if i == 6:
                    weigh_top()
                for r1, c1 in tail(MIXED, u):
                    mixture(r1, c1)
                for r1, c1 in tail(BASE1, u):
                    gate_base1(r1, c1)
            finish(U - 1)
            constants_lut(nc, v, dve)
            dve.wait_ge(v["idx_narrow"], 1)
            take_bits03(V, v, 0)
            for c1 in range(CC):
                mixture(R2 - 1, c1)
                if c1 >= 1:
                    gate_base1(R2 - 1, c1 - 1)
            gate_base1(R2 - 1, CC - 1)
            end_round(dve)


def take_bits03(V, v, p):
    V.tensor_scalar(v["bits03"][p][:, :], v["idx16"][p][:, :], 5, 0x100 + BIT0, ALU.logical_shift_left,
                    ALU.bitwise_and).then_inc(v["bits03_ready"], 1)


def narrow_idx(nc, v, p):
    nc.scalar.activation(v["idx16"][p][:, :], v["idx_sb"][p][:, :], ACT.Copy).then_inc(v["idx_narrow"], 1)


def block_lookup(nc, v):
    sb = v["sb"]
    (idx, wh, wl, lut_in, lut_d, hold) = (v[n] for n in "idx wh wl lut_in lut_d hold".split())
    (idx_in, idx_narrow, bits03_ready, bits12_ready, leaves_act, leaves_pool, pairs_done, fours_done, weight_full,
     weight_hi, weight_lo) = (v[n] for n in ("idx_in idx_narrow bits03_ready bits12_ready leaves_act leaves_pool "
                                             "pairs_done fours_done weight_full weight_hi weight_lo").split())
    begin_round, end_round, next_round = v["begin_round"], v["end_round"], v["next_round"]
    prod = Products(nc, v)
    ROUND = 1
    ACT_LEAVES = (2, 4, 6, 1, 0)
    POOL_LEAVES = (3, 5, 7)
    with ExitStack() as tmp:
        idx_sb, idx16, bits03 = v["idx_sb"], v["idx16"], v["bits03"]
        bits12 = [sb(f"bits12_{p}", [P, SB], I16, tmp) for p in range(2)]
        odd = [sb(f"leaf_{n}", [P, SB], F32, tmp) for n in (1, 3, 5, 7)]
        even = [[sb(f"leaf{p}_{n}", [P, SB], F32, tmp) for n in (0, 2, 4, 6)] for p in range(2)]
        x1b = [sb(f"x1b{c}", [P, T], F32, tmp) for c in range(CC)]

        def leaf(p, n):
            return odd[n // 2] if n % 2 else even[p][n // 2]

        def bit(p, n):
            pair = (bits12 if n in (1, 2) else bits03)[p][:, :].bitcast(U8).rearrange("p (n two) -> p n two", two=2)
            return pair[:, :, n // 2]

        wh_flat = wh[:, :, :].rearrange("p j n -> p (j n)")
        wl_flat = wl[:, :, :].rearrange("p j n -> p (j n)")
        idx_flat = idx.rearrange("s p n -> (s p) n")
        block = tmp.enter_context(nc.Block())

        def chunks(eng, step):
            def chunk(j, q):
                for part in range(3):
                    step(3 * j + part, (3 * q + part) % 2, j, q, part)
            for j in range(3):
                chunk(j, j % 2)
            with eng.Fori(0, (FJ - 3) // 2) as it:
                for jj in range(2):
                    chunk(2 * it + (3 + jj), 1 - jj)

        def at_least(j, n):
            return not isinstance(j, int) or j >= n

        @block.sync
        def _(sp):
            begin_round(sp, "sp", ROUND)
            prod.fetch_x1(sp, 0, x1b)
            load_k_ahead(v, sp, 2)

            def step(s, p, j, q, part):
                sp.wait_ge(idx_narrow, s + 1)
                sp.dma_start(idx_sb[p][:, :], idx_flat[bass.ds((s + 2) * P, P), :]).then_inc(idx_in[p], 16)

            chunks(sp, step)
            sp.wait_ge(idx_in[0], 16 * ((NS + 3) // 2))
            sp.wait_ge(idx_in[1], 16 * ((NS + 2) // 2))
            prod.store_y(sp, 0, x1b)
            sp.wait_ge(v["S"]["k_ahead"], 32)
            next_round(sp)

        def leaves(wait, of, s, p, which, done):
            wait(bits03_ready, s + 1)
            for n in which:
                sm, count = ((pairs_done, 4 * s - 4 + (n + 1) // 2) if n % 2 else
                             (weight_full, s - 1) if n else (weight_lo, s - 1))
                if not isinstance(count, int) or (count > 0 and s > 0):
                    wait(sm, count)
                args = (leaf(p, n)[:, :], bit(p, 0))
                if of is nc.scalar:
                    ins = of.activation(*args, ACT.Identity, bias=lut_in[:, 2 * n:2 * n + 1],
                                        scale=lut_d[:, n:n + 1])
                else:
                    ins = of.tensor_scalar(*args, lut_d[:, n:n + 1], lut_in[:, 2 * n:2 * n + 1], ALU.mult, ALU.add)
            ins.then_inc(done, 1)

        @block.scalar
        def _(act):
            def wait(sm, val):
                hold(act, "act", sm, val)

            def narrow(s, p):
                wait(idx_in[p], 8 * (s - p) + 16)
                narrow_idx(nc, v, p)

            begin_round(act, "act", ROUND)
            leaves(wait, nc.scalar, 0, 0, ACT_LEAVES, leaves_act)
            nc.scalar.preload_act_table_set("silu_and_others")

            def step(s, p, j, q, part):
                wait(bits12_ready, s + 1)
                narrow(s + 2, p)
                leaves(wait, nc.scalar, s + 1, 1 - p, ACT_LEAVES, leaves_act)
                if part == 0 and at_least(j, 1):
                    prod.silu(wait, j - 1, 1 - q, at_least(j, 3))
                if part == 1 and at_least(j, 1):
                    prod.split_hi(wait, j - 1, 1 - q, at_least(j, 3))
                wait(weight_full, s + 1)
                nc.scalar.activation(wh_flat[:, bass.ds(s * SB, SB)], leaf(p, 0)[:, :],
                                     ACT.Copy).then_inc(weight_hi, 1)

            chunks(act, step)
            prod.silu(wait, FJ - 1, (FJ - 1) % 2, True)
            prod.input_hi(act, True, fresh=False)
            prod.split_hi(wait, FJ - 1, (FJ - 1) % 2, True)
            end_round(act)

        @block.gpsimd
        def _(pool):
            def wait(sm, val):
                hold(pool, "pool", sm, val)

            begin_round(pool, "pool", ROUND)
            leaves(wait, nc.gpsimd, 0, 0, POOL_LEAVES, leaves_pool)

            def step(s, p, j, q, part):
                leaves(wait, nc.gpsimd, s + 1, 1 - p, POOL_LEAVES, leaves_pool)
                if part == 2 and at_least(j, 1):
                    prod.split_lo(wait, j - 1, 1 - q)
                wait(weight_hi, s + 1)
                nc.gpsimd.tensor_tensor(wl_flat[:, bass.ds(s * SB, SB)], leaf(p, 0)[:, :],
                                        wh_flat[:, bass.ds(s * SB, SB)].bitcast(F32), ALU.subtract).then_inc(weight_lo, 1)

            chunks(pool, step)
            prod.split_lo(wait, FJ - 1, (FJ - 1) % 2)
            prod.input_lo(pool, nc.gpsimd, (0, 2))
            end_round(pool)

        @block.tensor
        def _(pe):
            begin_round(pe, "pe", ROUND)
            for j in range(FJ):
                pe.wait_ge(weight_lo, 3 * j + 1)
                prod.gate(pe, j)
                pe.wait_ge(weight_lo, 3 * j + 2)
                prod.up(pe, j)
                if j >= 1:
                    prod.down(pe, j - 1)
            pe.wait_ge(weight_lo, 3 * FJ)
            prod.down(pe, FJ - 1)
            end_round(pe)

        @block.vector
        def _(dve):
            V = nc.vector

            def wait(sm, val):
                hold(dve, "dve", sm, val)

            def select(p, a, n):
                return V.copy_predicated(leaf(p, a)[:, :], bit(p, n), leaf(p, a + (1 << (n - 1)))[:, :])

            def take_bits12(s, p):
                V.tensor_scalar(bits12[p][:, :], idx16[p][:, :], 6, 0x180, ALU.logical_shift_left,
                                ALU.bitwise_and).then_inc(bits12_ready, 1)

            begin_round(dve, "dve", ROUND)
            take_bits12(0, 0)

            def step(s, p, j, q, part):
                wait(bits12_ready, s + 1)
                wait(leaves_act, s + 1)
                wait(leaves_pool, s + 1)
                select(p, 0, 1).then_inc(pairs_done, 1)
                wait(idx_narrow, s + 2)
                if at_least(s, 1):
                    wait(weight_full, s)
                take_bits03(V, v, 1 - p)
                for a in (2, 4, 6):
                    select(p, a, 1).then_inc(pairs_done, 1)
                wait(pairs_done, 4 * s + 2)
                select(p, 0, 2).then_inc(fours_done, 1)
                if part == 1 and at_least(j, 1):
                    prod.hidden(wait, j - 1, 1 - q)
                wait(pairs_done, 4 * s + 4)
                select(p, 4, 2).then_inc(fours_done, 1)
                take_bits12(s + 1, 1 - p)
                wait(fours_done, 2 * s + 2)
                select(p, 0, 3).then_inc(weight_full, 1)

            chunks(dve, step)
            prod.hidden(wait, FJ - 1, (FJ - 1) % 2)
            prod.input_lo(dve, V, (1, 3))
            prod.add_x1(dve, x1b)
            end_round(dve)


def block_rounds(nc, v, rounds):
    sb, S, hold = v["sb"], v["S"], v["hold"]
    begin_round, end_round, next_round = v["begin_round"], v["end_round"], v["next_round"]
    (x, k, x1_dram, rw, rb, eb, ones, ident, u_in, dec, osc, base1) = (
        v[n] for n in "x k x1_dram rw rb eb ones ident u_in dec osc base1".split())
    ps_a, ps_b, y_out = v["ps_a"], v["ps_b"], v["y_out"]
    prod = Products(nc, v)
    with ExitStack() as tmp:
        def t(name, shape, dt=F32):
            return sb(f"{name}_rounds", shape, dt, tmp)

        dec_cur, osc_cur, kb = v["dec_cur"], v["osc_cur"], v["kb"]
        base0 = t("base0", [P, CC, T])
        ek = [t(f"ek{p}", [P, T]) for p in range(2)]
        ekv = [t(f"ekv{p}", [P, T]) for p in range(2)]
        eu = [t(f"eu{p}", [P, T]) for p in range(2)]
        fd = [t(f"fd{p}", [P, T]) for p in range(2)]
        bd = [t(f"bd{p}", [P, T]) for p in range(2)]
        fn = [t(f"fn{p}", [P, T]) for p in range(2)]
        bn = [t(f"bn{p}", [P, T]) for p in range(2)]
        xs = [v["idx_sb"][p][:, :].bitcast(F32) for p in range(2)]
        top8 = t("top8", [P, TT, 8])
        neg_max = t("neg_max", [P, TT])
        zsum = t("zsum", [P, TT])
        zinv = t("zinv", [P, TT])
        logits = fd[0][:, 0:TT * E].rearrange("p (t e) -> p t e", e=E)
        marked = fd[0][:, TT * E:2 * TT * E].rearrange("p (t e) -> p t e", e=E)
        exps = bd[0][:, 0:TT * E].rearrange("p (t e) -> p t e", e=E)
        picked = bd[0][:, TT * E:2 * TT * E].rearrange("p (t e) -> p t e", e=E)
        picked_t = bn[0][0:E, :]
        x1b = [fd[1], bd[1], fn[1], bn[1]]

        block = tmp.enter_context(nc.Block())

        def run(eng, body):
            for number, g, r in rounds:
                if number == "loop":
                    first, count = g, r
                    with eng.Fori(0, count) as it:
                        body(it + first, it + (first - 1), it + first)
                else:
                    body(number, g, r)

        @block.sync
        def _(sp):
            def store_x1(r, c):
                sp.wait_ge(S["x1_ready"], c + 1)
                sp.dma_start(row(x1_dram, r, c), xs[c % 2][:, :]).then_inc(S[f"x1_out{c % 2}"], 16)

            def body(number, g, r):
                begin_round(sp, "sp", number)
                if r is not None:
                    for c in range(CC):
                        sp.dma_start(base0[:, c, :], row(x, r, c)).then_inc(S[f"x_in{c}"], 16)
                if r is not None:
                    for c in range(2):
                        sp.dma_start(xs[c][:, :], row(x, r, c)).then_inc(S[f"xb_in{c}"], 16)
                    for c in range(2, CC):
                        sp.wait_ge(S["lifted"], 2 * (c - 1))
                        sp.wait_ge(S["ekv_ready"], c - 1)
                        sp.dma_start(kb[c % 2][:, :], row(k, r, c)).then_inc(S[f"k_in{c % 2}"], 16)
                    sp.wait_ge(S["ratio_done"], HU)
                    prod.fetch_x1(sp, g, x1b)
                    load_k_ahead(v, sp, r + 1)
                    for c in range(CC):
                        if c >= 2:
                            sp.wait_ge(S[f"x1_out{c % 2}"], 16)
                            sp.wait_ge(S["t1_ready"], c - 1)
                            sp.dma_start(xs[c % 2][:, :], row(x, r, c)).then_inc(S[f"xb_in{c % 2}"], 16)
                        if c >= 1:
                            store_x1(r, c - 1)
                    store_x1(r, CC - 1)
                if r is None:
                    prod.fetch_x1(sp, g, x1b)
                prod.store_y(sp, g, x1b)
                if r is not None:
                    sp.wait_ge(S["k_ahead"], 32)
                    sp.wait_ge(S["x1_out0"], 32)
                    sp.wait_ge(S["x1_out1"], 32)
                next_round(sp)

            sp.wait_ge(y_out, 16 * CC)
            run(sp, body)
            sp.wait_ge(y_out, 16 * B * CC)

        @block.scalar
        def _(act):
            def ek_of(c):
                act.wait_ge(S["k_capped"], c + 1)
                nc.scalar.activation(ek[c % 2][:, :], ek[c % 2][:, :], ACT.Exp).then_inc(S["ek_ready"], 1)

            def eu_of(i):
                c, layer = divmod(i, 2)
                if layer == 0 and c >= 2:
                    act.wait_ge(S[f"k_in{c % 2}"], 16)
                if i >= 2:
                    act.wait_ge(S["num_full"], i - 1)
                n = layer * CC + c
                nc.scalar.activation(eu[i % 2][:, :], kb[c % 2][:, :], ACT.Exp,
                                     bias=u_in[:, n:n + 1]).then_inc(S["e_ready"], 1)

            def tanh_x(c):
                act.wait_ge(S[f"x_in{c}"], 16)
                nc.scalar.activation(base0[:, c, :], base0[:, c, :], ACT.Tanh, scale=0.5).then_inc(S["t0_ready"], 1)

            def body(number, g, r):
                G, R = g is not None, r is not None
                begin_round(act, "act", number)
                if R:
                    nc.scalar.preload_act_table_set("natural_log_exp_and_others")
                    ek_of(0)
                    eu_of(0)
                    eu_of(1)
                for j in range(FJ + 1):
                    rec = R and j < HU
                    if G and j >= 1:
                        prod.split_hi(act.wait_ge, j - 1, (j - 1) % 2, j >= 3)
                    if rec and 0 < j < HU - 1:
                        eu_of(j + 1)
                        if j % 2 == 1:
                            ek_of(j // 2 + 1)
                    if R and j == 8:
                        act.wait_ge(S["top_done"], 1)
                        for n in range(TT):
                            ins = nc.scalar.activation(exps[:, n, :], logits[:, n, :], ACT.Exp,
                                                       bias=neg_max[:, n:n + 1], accum_out=zsum[:, n:n + 1])
                        ins.then_inc(S["exps_done"], 1)
                    if R and j == 9:
                        act.wait_ge(S["pick_done"], 1)
                        nc.scalar.activation(picked_t, ps_b[0:E, :], ACT.Copy).then_inc(S["picked_t"], 1)
                    if G and j < FJ:
                        prod.silu(act.wait_ge, j, j % 2, j >= 2)
                    if G and R and j < CC:
                        tanh_x(j)
                    if R and j in (9, 10, 11):
                        for c1 in {9: (0, 1), 10: (2, 3), 11: ()}[j]:
                            act.wait_ge(S["x1_ready"], c1 + 1)
                            nc.scalar.activation(base0[:, c1, :], xs[c1 % 2][:, :], ACT.Tanh,
                                                 scale=0.5).then_inc(S["t1_ready"], 1)
                    if rec:
                        if G:
                            nc.scalar.preload_act_table_set("natural_log_exp_and_others")
                        act.wait_ge(S["den_ready"], j + 1)
                        nc.scalar.activation(fd[j % 2][:, :], bd[j % 2][:, :], ACT.Ln).then_inc(S["ln_done"], 1)
                        act.wait_ge(S["ln_done"], j + 1)
                        nc.scalar.activation(fd[j % 2][:, :], fd[j % 2][:, :], ACT.Exp,
                                             scale=-1.0).then_inc(S["recip_done"], 1)
                if R:
                    prod.input_hi(act, True, fresh=True)
                end_round(act)

            run(act, body)

        @block.gpsimd
        def _(pool):
            def refine(i):
                pool.wait_ge(S["recip_done"], i + 1)
                nc.gpsimd.tensor_tensor(bd[i % 2][:, :], bd[i % 2][:, :], fd[i % 2][:, :],
                                        ALU.mult).then_inc(S["newton"], 1)

            def weigh(c):
                pool.wait_ge(S["ek_ready"], c + 1)
                if c >= 2:
                    pool.wait_ge(S["num_scans"], 4 * (c - 1))
                nc.gpsimd.tensor_tensor(ekv[c % 2][:, :], ek[c % 2][:, :], kb[c % 2][:, :],
                                        ALU.mult).then_inc(S["ekv_ready"], 1)

            def body(number, g, r):
                G, R = g is not None, r is not None
                begin_round(pool, "pool", number)
                if R:
                    weigh(0)
                for j in range(FJ + 1):
                    c, layer = divmod(j, 2)
                    q = j % 2
                    rec = R and j < HU
                    if G and j >= 1:
                        prod.split_lo(pool.wait_ge, j - 1, (j - 1) % 2)
                    if rec:
                        pool.wait_ge(S["den_part"], j + 1)
                        nc.gpsimd.tensor_tensor(fd[q][:, 0:T - 1], fd[q][:, 0:T - 1], bd[q][:, 0:T - 1],
                                                ALU.add).then_inc(S["den_sum"], 1)
                    if R and 1 <= j <= HU:
                        refine(j - 1)
                    if rec:
                        pool.wait_ge(S["num_scans"], 2 * (j + 1))
                        nc.gpsimd.tensor_tensor(fn[q][:, 0:T - 1], fn[q][:, 0:T - 1], bn[q][:, 0:T - 1],
                                                ALU.add).then_inc(S["num_sum"], 1)
                        pool.wait_ge(S["num_sum"], j + 1)
                        pool.wait_ge(S["lifted"], j + 1)
                        nc.gpsimd.tensor_tensor(fn[q][:, :], fn[q][:, :], eu[q][:, :],
                                                ALU.add).then_inc(S["num_full"], 1)
                        if layer == 1 and c + 1 < CC:
                            weigh(c + 1)
                    if R and j in (9, 10, 11):
                        for c1 in {9: (0, 1), 10: (2, 3), 11: ()}[j]:
                            pool.wait_ge(S["mixed"], c1 + 1)
                            pool.wait_ge(S[f"xb_in{c1 % 2}"], 16 * (c1 // 2 + 1))
                            nc.gpsimd.tensor_tensor(xs[c1 % 2][:, :], base0[:, c1, :], xs[c1 % 2][:, :],
                                                    ALU.add).then_inc(S["x1_ready"], 1)
                if R:
                    prod.input_lo(pool, nc.gpsimd, (0, 2))
                end_round(pool)

            run(pool, body)

        @block.tensor
        def _(pe):
            def mix(c):
                if c == 0:
                    pe.wait_ge(S["picked_t"], 1)
                else:
                    pe.wait_ge(S["mixed"], c)
                nc.tensor.matmul(ps_b[:, :], eb[:, c * P:(c + 1) * P], picked_t, start=True,
                                 stop=True).then_inc(S["mix_done"], 1)

            def body(number, g, r):
                G, R = g is not None, r is not None
                begin_round(pe, "pe", number)
                for j in range(FJ):
                    if R and j == 9:
                        pe.wait_ge(S["picked_t"], 1)
                        nc.tensor.matmul(ps_a[:, :], ones[0:E, :], picked_t, start=True,
                                         stop=True).then_inc(S["spread_done"], 1)
                        mix(0)
                    if R and j == 10:
                        mix(2)
                    if G:
                        prod.gate(pe, j)
                    if R and j == 9:
                        mix(1)
                    if R and j == 10:
                        mix(3)
                    if G:
                        prod.up(pe, j)
                    if R and j == 7:
                        pe.wait_ge(S["base0_ready"], CC)
                        for n in range(TT):
                            for c in range(CC):
                                ins = nc.tensor.matmul(ps_a[:, n * E:(n + 1) * E], base0[:, c, n * P:(n + 1) * P],
                                                       rw[:, c, :], start=c == 0, stop=c == CC - 1)
                        ins.then_inc(S["logits_done"], 1)
                    if R and j == 8:
                        pe.wait_ge(S["picked"], 1)
                        for n in range(TT):
                            ins = nc.tensor.transpose(ps_b[0:E, n * P:(n + 1) * P], picked[:, n, :], ident[:, :])
                        ins.then_inc(S["pick_done"], 1)
                    if G and j >= 1:
                        prod.down(pe, j - 1)
                if G:
                    prod.down(pe, FJ - 1)
                end_round(pe)

            run(pe, body)

        @block.vector
        def _(dve):
            V = nc.vector

            def cap(c):
                if c >= 2:
                    dve.wait_ge(S[f"k_in{c % 2}"], 16)
                    dve.wait_ge(S["ekv_ready"], c - 1)
                V.tensor_scalar(ek[c % 2][:, :], kb[c % 2][:, :], KMAX, None, ALU.min).then_inc(S["k_capped"], 1)

            def scan_pair(src, fwd, bwd, d, done):
                V.tensor_tensor_scan(fwd[:, :], d.to_broadcast([P, T]), src[:, :], 0.0, ALU.mult,
                                     ALU.add).then_inc(done, 1)
                V.tensor_tensor_scan(bwd[:, T - 2::-1], src[:, T - 1:0:-1], d.to_broadcast([P, T - 1]), 0.0, ALU.add,
                                     ALU.mult).then_inc(done, 1)

            def finish(i):
                c, layer = divmod(i, 2)
                q = i % 2
                dve.wait_ge(S["num_full"], i + 1)
                dve.wait_ge(S["recip_done"], i + 1)
                V.scalar_tensor_tensor(out=fn[q][:, :], in0=fn[q][:, :], scalar=osc_cur[:, 0:1], in1=fd[q][:, :],
                                       op0=ALU.mult, op1=ALU.mult).then_inc(S["quotient"], 1)
                dve.wait_ge(S["quotient"], i + 1)
                dve.wait_ge(S["newton"], i + 1)
                dst = (fn[q][:, :], base1[:, c, :])[layer]
                V.scalar_tensor_tensor(out=dst, in0=bd[q][:, :], scalar=2.0, in1=fn[q][:, :], op0=ALU.subtract,
                                       op1=ALU.mult).then_inc(S["ratio_done"], 1)
                if layer == 0:
                    dve.wait_ge(S["ratio_done"], i + 1)
                    dve.wait_ge(S["t0_ready"], c + 1)
                    V.scalar_tensor_tensor(out=base0[:, c, :], in0=base0[:, c, :], scalar=1.0, in1=dst, op0=ALU.add,
                                           op1=ALU.mult).then_inc(S["base0_ready"], 1)

            def recurrence(j, G, g):
                c, layer = divmod(j, 2)
                q = j % 2
                d = dec_cur[:, layer * CC + c:layer * CC + c + 1]
                if G and j == 1:
                    hold(dve, "dve", y_out, 16 * CC * g)
                if j >= 2:
                    dve.wait_ge(S["ratio_done"], j - 1)
                    dve.wait_ge(S["base0_ready"], (j - 1 + 1) // 2)
                dve.wait_ge(S["ek_ready"], c + 1)
                scan_pair(ek[c % 2], fd[q], bd[q], d, S["den_scans"])
                dve.wait_ge(S["den_scans"], 2 * j + 2)
                dve.wait_ge(S["e_ready"], j + 1)
                V.scalar_tensor_tensor(out=fd[q][:, :], in0=eu[q][:, :], scalar=EXP_KMAX, in1=fd[q][:, :],
                                       op0=ALU.min, op1=ALU.add).then_inc(S["den_part"], 1)
                V.scalar_tensor_tensor(out=eu[q][:, :], in0=eu[q][:, :], scalar=EXP_KMAX, in1=kb[c % 2][:, :],
                                       op0=ALU.min, op1=ALU.mult).then_inc(S["lifted"], 1)
                dve.wait_ge(S["ekv_ready"], c + 1)
                scan_pair(ekv[c % 2], fn[q], bn[q], d, S["num_scans"])
                if j >= 1:
                    finish(j - 1)
                dve.wait_ge(S["den_sum"], j + 1)
                V.tensor_scalar(bd[q][:, :], fd[q][:, :], DEN_MIN, None, ALU.max).then_inc(S["den_ready"], 1)
                if layer == 0 and c + 1 < CC:
                    cap(c + 1)

            def body(number, g, r):
                G, R = g is not None, r is not None
                begin_round(dve, "dve", number)
                if R:
                    V.tensor_copy(dec_cur[:, :], dec[:, bass.ds(r, 1), :].rearrange("p b n -> p (b n)")
                                  ).then_inc(S["cur_ready"], 1)
                    V.tensor_copy(osc_cur[:, :], osc[:, bass.ds(r, 1)]).then_inc(S["cur_ready"], 1)
                    cap(0)
                    dve.wait_ge(S["cur_ready"], 2)
                for j in range(FJ + 1):
                    if G and j >= 1:
                        prod.hidden(dve.wait_ge, j - 1, (j - 1) % 2)
                    if R and j < HU:
                        recurrence(j, G, g)
                    if R and j == HU:
                        finish(HU - 1)
                        top_k()
                    if R and j in (9, 10, 11):
                        for c1 in {9: (0, 1), 10: (2, 3), 11: ()}[j]:
                            mixture(c1)
                        for c1 in {9: (), 10: (0, 1), 11: (2, 3)}[j]:
                            dve.wait_ge(S["t1_ready"], c1 + 1)
                            V.scalar_tensor_tensor(out=base1[:, c1, :], in0=base0[:, c1, :], scalar=1.0,
                                                   in1=base1[:, c1, :], op0=ALU.add,
                                                   op1=ALU.mult).then_inc(S["base1_ready"], 1)
                if R:
                    prod.input_lo(dve, V, (1, 3))
                if G:
                    prod.add_x1(dve, x1b)
                end_round(dve)

            def top_k():
                chain = [0]

                def link(ins):
                    chain[0] += 1
                    ins.then_inc(S["l0_chain"], 1)

                def linked():
                    dve.wait_ge(S["l0_chain"], chain[0])

                dve.wait_ge(S["logits_done"], 1)
                dve.wait_ge(S["ratio_done"], HU)
                link(V.tensor_tensor(logits, ps_a[:, 0:TT * E].rearrange("p (t e) -> p t e", e=E),
                                     rb[:, None, :].to_broadcast([P, TT, E]), ALU.add))
                linked()
                for n in range(TT):
                    link(V.max(top8[:, n, :], logits[:, n, :]))
                linked()
                V.tensor_scalar(neg_max[:, :], top8[:, :, 0], -1.0, None, ALU.mult).then_inc(S["top_done"], 1)
                for n in range(TT):
                    link(V.match_replace(marked[:, n, :], top8[:, n, :], logits[:, n, :], TAKEN))
                linked()
                link(V.tensor_tensor(marked, marked, logits, ALU.not_equal))
                dve.wait_ge(S["exps_done"], 1)
                link(V.reciprocal(zinv[:, :], zsum[:, :]))
                linked()
                link(V.tensor_tensor(picked, marked, exps, ALU.mult))
                linked()
                V.tensor_tensor(picked, picked, zinv[:, :, None].to_broadcast([P, TT, E]),
                                ALU.mult).then_inc(S["picked"], 1)

            def mixture(c):
                if c == 0:
                    dve.wait_ge(S["spread_done"], 1)
                V.tensor_tensor(base0[:, c, :], base0[:, c, :], ps_a[:, :], ALU.mult).then_inc(S["mix_half"], 1)
                dve.wait_ge(S["mix_half"], c + 1)
                dve.wait_ge(S["mix_done"], c + 1)
                V.tensor_tensor(base0[:, c, :], base0[:, c, :], ps_b[:, :], ALU.add).then_inc(S["mixed"], 1)

            hold(dve, "dve", y_out, 16 * CC)
            run(dve, body)


def load_k_ahead(v, sp, r):
    for c in range(2):
        sp.dma_start(v["kb"][c][:, :], row(v["k"], r, c)).then_inc(v["S"]["k_ahead"], 16)


def load_constants(nc, v, sp, late):
    small = {"cond": v["cond_t"], "w": v["w_in"], "u": v["u_in"]}
    big = {"lut": v["lut_in"], "router_b": v["rb"], "expert_b": v["eb"], "router_w": v["rw"]}
    for n, dst in (big if late else small).items():
        src = v[n]
        if n in ("lut", "router_b"):
            src = src.to_broadcast([P, src.shape[1]])
        if n == "router_w":
            sp.dma_start(dst[:, :, :], src).then_inc(v["late_consts_in"], 16)
        elif late:
            sp.dma_start(dst[:, :], src).then_inc(v["late_consts_in"], 16)
        else:
            sp.dma_start(dst[:, :], src).then_inc(v["consts_in"], 16)


def constants_act(nc, v, act):
    tf, dec0, ps_a, w_in, setup_exp = (v[n] for n in "tf dec0 ps_a w_in setup_exp".split())
    act.wait_ge(v["consts_in"], 48)
    act.wait_ge(v["cond_sum"], 1)
    nc.scalar.activation(tf[:, 0, :], ps_a[:, 0:B], ACT.Exp, scale=-1.0).then_inc(setup_exp, 1)
    nc.scalar.activation(dec0[:, 0, :], w_in[:, :], ACT.Exp).then_inc(setup_exp, 1)
    act.wait_ge(setup_exp, 2)
    nc.scalar.activation(dec0[:, 1, :], dec0[:, 0, :], ACT.Exp, scale=-1.0).then_inc(setup_exp, 1)


def constants_pool(nc, v, pool):
    ones, ident, pool_consts = (v[n] for n in "ones ident pool_consts".split())
    nc.gpsimd.memset(ones[:, :], 1.0).then_inc(pool_consts, 1)
    nc.gpsimd.memset(ident[:, :], 0.0).then_inc(pool_consts, 1)
    pool.wait_ge(pool_consts, 2)
    nc.gpsimd.affine_select(out=ident[:, :], in_=ident[:, :], compare_op=ALU.not_equal, fill=1.0, base=0,
                            pattern=[[-1, P]], channel_multiplier=1).then_inc(pool_consts, 1)


def constants_pe(nc, v, pe):
    pe.wait_ge(v["consts_in"], 48)
    pe.wait_ge(v["pool_consts"], 3)
    nc.tensor.matmul(v["ps_a"][:, 0:B], v["ones"][:, :], v["cond_t"][:, :], start=True,
                     stop=True).then_inc(v["cond_sum"], 1)


def constants_dve(nc, v, dve, late):
    tf, dec, dec0, osc, osc2, setup_dve = (v[n] for n in "tf dec dec0 osc osc2 setup_dve".split())
    chain = [4 if late else 0]

    def link(ins):
        chain[0] += 1
        ins.then_inc(setup_dve, 1)
        dve.wait_ge(setup_dve, chain[0])

    def decay(b):
        link(nc.vector.tensor_scalar(dec[:, b, :], dec0[:, 1, :], tf[:, 3, b:b + 1], None, ALU.mult))

    if not late:
        dve.wait_ge(v["setup_exp"], 3)
        link(nc.vector.tensor_scalar(tf[:, 1, :], tf[:, 0, :], 1.0, None, ALU.add))
        link(nc.vector.reciprocal(tf[:, 2, :], tf[:, 1, :]))
        link(nc.vector.tensor_scalar(tf[:, 3, :], tf[:, 2, :], 0.5, 0.5, ALU.mult, ALU.add))
        decay(0)
    else:
        link(nc.vector.tensor_scalar(osc2[:, :], tf[:, 2, :], -0.2, -0.8, ALU.mult, ALU.add))
        link(nc.vector.tensor_scalar(osc[:, :], tf[:, 2, :], -0.1, -0.4, ALU.mult, ALU.add))
        for b in range(1, B):
            decay(b)


def constants_lut(nc, v, dve):
    lut_d, lut_in, lut_diff = v["lut_d"], v["lut_in"], v["lut_diff"]
    dve.wait_ge(v["late_consts_in"], 64)
    pair = lut_in[:, :].rearrange("p (n two) -> p n two", two=2)
    nc.vector.tensor_tensor(lut_d[:, :], pair[:, :, 1], pair[:, :, 0], ALU.subtract).then_inc(lut_diff, 1)
    dve.wait_ge(lut_diff, 1)
    nc.vector.tensor_scalar(lut_d[:, :], lut_d[:, :], 1.0 / BIT0, None, ALU.mult)


def kernel(**inputs):
    import numpy as np
    import concourse.bacc as bacc
    from concourse.bass_utils import run_bass_kernel_spmd

    a = {n: np.asarray(v) for n, v in inputs.items()}

    def columns(v):
        return v.reshape(CC, P).T

    def chunked(idx):
        idx = np.pad(idx, ((0, FJ * P - F), (0, 0)))
        return idx.reshape(FJ, P, CC, P).transpose(0, 3, 2, 1).reshape(FJ, P, CC * P)

    down = np.pad(a["L1_ffn_down_idx"], ((0, 0), (0, FJ * P - F))).T.reshape(FJ, P, C)
    idx = np.concatenate([chunked(a["L1_ffn_gate_idx"]), chunked(a["L1_ffn_up_idx"]), down], axis=2)
    idx = idx.reshape(FJ, P, WJ // SB, SB).transpose(0, 2, 1, 3).reshape(NS, P, SB)
    idx = np.pad(idx, ((0, 2), (0, 0), (0, 0)))
    arrays = {
        "x": a["x"].transpose(0, 2, 1).reshape(B, CC, P, T),
        "k": np.pad(a["fside_BxSxS_0"].transpose(0, 2, 1).reshape(B, CC, P, T), ((0, 1), (0, 0), (0, 0), (0, 0))),
        "cond": a["cond_512"].T,
        "w": np.concatenate([columns(a["L0_cond_w"]), columns(a["L1_cond_w"])], axis=1),
        "u": np.concatenate([columns(a["L0_cond_u"]), columns(a["L1_cond_u"])], axis=1),
        "router_w": a["L0_ffn_router_weight"].T.reshape(CC, P, E).transpose(1, 0, 2),
        "router_b": a["L0_ffn_router_bias"].reshape(1, E),
        "expert_b": a["L0_ffn_expert_bias"],
        "lut": a["L1_ffn_lut"].reshape(1, 16),
        "idx": idx,
    }
    arrays = {n: np.ascontiguousarray(v) for n, v in arrays.items()}
    nc = bacc.Bacc("TRN2", target_bir_lowering=False, num_devices=1, dynamic_dma_scratch_size=1024)
    aps = {n: nc.dram_tensor(f"in_{n}", v.shape, mybir.dt.from_np(v.dtype), kind="ExternalInput").ap()
           for n, v in arrays.items()}
    y = nc.dram_tensor("y", (B, CC, P, T), F32, kind="ExternalOutput").ap()
    build(nc, y=y, **aps)
    r = run_bass_kernel_spmd(nc, [{f"in_{n}": v for n, v in arrays.items()}], core_ids=[0])
    out = r.results[0]["y"]
    return np.ascontiguousarray(out.reshape(B, C, T).transpose(0, 2, 1))
```

```python
from contextlib import ExitStack

import concourse.bass as bass
from concourse import mybir

F32 = mybir.dt.float32
F32R = mybir.dt.float32r
I32 = mybir.dt.int32
I16 = mybir.dt.int16
U8 = mybir.dt.uint8
ALU = mybir.AluOpType
ACT = mybir.ActivationFunctionType

P = 128
B, T, C = 4, 512, 512
CC = C // P
E = 64
TT = T // P
F = 1376
FJ = -(-F // P)
FLAST = F - (FJ - 1) * P
WJ = 3 * CC * P
SB = CC * P
NS = FJ * WJ // SB
HU = 2 * CC
KMAX = 30.0
EXP_KMAX = 1.0686474581524463e13
DEN_MIN = 1e-8
BIT0 = 0x20
TAKEN = -3.0e38


def build(nc, x, k, cond, w, u, router_w, router_b, expert_b, lut, idx, y):
    ctx = ExitStack()
    with ctx:
        def sb(name, shape, dt=F32, into=ctx):
            return into.enter_context(nc.sbuf_tensor(name, shape, dt))

        def ps(name):
            return ctx.enter_context(nc.psum_tensor(name, [P, T], F32))

        def sem(name):
            return ctx.enter_context(nc.semaphore(name))

        x1_dram = nc.dram_tensor("x1_scratch", (B, CC, P, T), F32, kind="Internal").ap()

        xh = sb("xh", [P, CC, T], F32R)
        xl = sb("xl", [P, CC, T], F32R)
        base1 = sb("base1", [P, CC, T])
        act_h = [sb(f"act_h{p}", [P, T]) for p in range(2)]
        hh = [sb(f"hh{p}", [P, T], F32R) for p in range(2)]
        hl = [sb(f"hl{p}", [P, T], F32R) for p in range(2)]
        rw = sb("rw", [P, CC, E])
        rb = sb("rb", [P, E])
        ebh = sb("ebh", [E, C], F32R)
        ebl = sb("ebl", [E, C], F32R)
        ones_r = sb("ones_r", [E, P], F32R)
        ones = sb("ones", [P, P])
        ident = sb("ident", [P, P])
        cond_t = sb("cond_t", [P, B])
        w_in = sb("w_in", [P, 2 * CC])
        u_in = sb("u_in", [P, 2 * CC])
        tf = sb("tf", [P, 4, B])
        dec0 = sb("dec0", [P, 2, 2 * CC])
        dec = sb("dec", [P, B, 2 * CC])
        osc = sb("osc", [P, B])
        osc2 = sb("osc2", [P, B])
        dec_cur = sb("dec_cur", [P, 2 * CC])
        osc_cur = sb("osc_cur", [P, 1])
        kb = [sb(f"kb{p}", [P, T]) for p in range(2)]
        idx_sb = [sb(f"idx_sb{p}", [P, SB], I32) for p in range(2)]
        idx_parts = sb("idx_parts", [P, 2, 2, SB], I16)
        idx16 = [idx_parts[:, 0, p, :] for p in range(2)]
        bits03 = [idx_parts[:, 1, p, :] for p in range(2)]
        lut_in = sb("lut_in", [P, 16])
        lut_d = sb("lut_d", [P, 8])
        ps_g, ps_u, ps_a, ps_b = ps("ps_g"), ps("ps_u"), ps("ps_a"), ps("ps_b")
        ps_d = [ps(f"ps_d{c}") for c in range(CC)]

        consts_in = sem("consts_in")
        late_consts_in = sem("late_consts_in")
        pool_consts = sem("pool_consts")
        cond_sum = sem("cond_sum")
        setup_exp = sem("setup_exp")
        setup_dve = sem("setup_dve")
        eb_hi = sem("eb_hi")
        eb_lo = sem("eb_lo")
        lut_diff = sem("lut_diff")
        round_done = sem("round_done")
        go = sem("go")
        held = {n: sem(f"held_{n}") for n in ("act", "dve", "pool", "pe", "sp")}
        idx_in = [sem("idx_in0"), sem("idx_in1")]
        idx_narrow = sem("idx_narrow")
        bits03_ready = sem("bits03_ready")
        bits12_ready = sem("bits12_ready")
        leaves_act = sem("leaves_act")
        leaves_pool = sem("leaves_pool")
        pairs_done = sem("pairs_done")
        fours_done = sem("fours_done")
        weight_full = sem("weight_full")
        weight_hi = sem("weight_hi")
        weight_lo = sem("weight_lo")
        y_out = sem("y_out")
        names = """
            k_ahead k_in0 k_in1 x_in0 x_in1 x_in2 x_in3 xb_in0 xb_in1 x1_out0 x1_out1 x1_back cur_ready
            k_capped ek_ready ekv_ready e_ready e_capped t0_ready den_scans den_part den_sum den_ready
            num_scans num_half lifted num_sum num_full ln_done recip_done newton quotient ratio_done base0_ready
            logits_done l0_chain top_done exps_done picked pick_done picked_hi picked_lo
            spread_done mix_done mix_half mixed x1_ready t1_ready base1_ready x_hi
            gate_done up_done silu_done h_full h_hi h_lo last_h_lo down_done bank_done down_used
            """.split()
        S = {n: sem(n) for n in names}
        nums = sorted(s.num for s in S.values())
        assert nums == list(range(nums[0], nums[0] + len(nums)))
        cleared = range(nums[0], nums[-1] + 1)

        def hold(eng, name, s, value):
            eng.wait_ge(s, value)
            eng.sem_inc(held[name], 1)

        def begin_round(eng, name, n):
            if not isinstance(n, int) or n > 0:
                hold(eng, name, go, n)

        def end_round(eng):
            eng.drain().then_inc(round_done, 1)

        def next_round(sp):
            sp.wait_ge(round_done, 4)
            sp.sem_clear(cleared)
            sp.sem_clear(round_done)
            sp.sem_inc(go, 1)

        k_first = [[sem(f"k_first{r}{c}") for c in range(CC)] for r in range(2)]
        x1_first = [sem(f"x1_first{c}") for c in range(CC)]
        x_first = [[sem(f"x_first{r}{c}") for c in range(CC)] for r in range(2)]

        v = dict(locals())
        block_first(nc, v)
        v["wh"] = sb("wh", [P, FJ, WJ], F32R)
        v["wl"] = sb("wl", [P, FJ, WJ], F32R)
        block_lookup(nc, v)
        block_rounds(nc, v, [("loop", 2, B - 2), (B, B - 1, None)])


def row(a, b, c):
    return a.rearrange("b c p t -> (b c p) t")[bass.ds((b * CC + c) * P, P), :]


class Products:

    def __init__(self, nc, v):
        self.nc, self.S = nc, v["S"]
        self.v = v

    def exact(self, out, terms):
        ops = [(a, m) for (ah, al, mh, ml) in terms for (a, m) in ((ah, mh), (al, mh), (ah, ml))]
        for n, (a, m) in enumerate(ops):
            ins = self.nc.tensor.matmul(out, a, m, start=n == 0, stop=n == len(ops) - 1)
        return ins

    def into_hidden(self, j, off, out):
        wh, wl, xh, xl = (self.v[n] for n in ("wh", "wl", "xh", "xl"))
        return self.exact(out, [(wh[:, j, off + c * P:off + (c + 1) * P], wl[:, j, off + c * P:off + (c + 1) * P],
                                 xh[:, c, :], xl[:, c, :]) for c in range(CC)])

    def gate(self, pe, j):
        if j >= 1:
            pe.wait_ge(self.S["silu_done"], j)
        self.into_hidden(j, 0, self.v["ps_g"][:, :]).then_inc(self.S["gate_done"], 1)

    def up(self, pe, j):
        if j >= 1:
            pe.wait_ge(self.S["h_full"], j)
        self.into_hidden(j, CC * P, self.v["ps_u"][:, :]).then_inc(self.S["up_done"], 1)

    def down(self, pe, j):
        wh, wl, hh, hl, ps_d = (self.v[n] for n in ("wh", "wl", "hh", "hl", "ps_d"))
        if j < FJ - 1:
            pe.wait_ge(self.S["h_lo"], j + 1)
        else:
            pe.wait_ge(self.S["last_h_lo"], 1)
        K = P if j < FJ - 1 else FLAST
        for c in range(CC):
            s = slice((2 * CC + c) * P, (2 * CC + c + 1) * P)
            for n, (a, m) in enumerate(((wh, hh), (wl, hh), (wh, hl))):
                ins = self.nc.tensor.matmul(ps_d[c][:, :], a[0:K, j, s], m[j % 2][0:K, :],
                                            start=(j == 0 and n == 0), stop=(j == FJ - 1 and n == 2))
            if j == FJ - 1:
                ins.then_inc(self.S["bank_done"], 1)
        if j < FJ - 1:
            ins.then_inc(self.S["down_done"], 1)

    def silu(self, wait, j, q, reused):
        wait(self.S["gate_done"], j + 1)
        if reused:
            wait(self.S["h_lo"], j - 1)
        self.nc.scalar.activation(self.v["act_h"][q][:, :], self.v["ps_g"][:, :],
                                  ACT.Silu).then_inc(self.S["silu_done"], 1)

    def hidden(self, wait, j, q):
        wait(self.S["silu_done"], j + 1)
        wait(self.S["up_done"], j + 1)
        h = self.v["act_h"][q][:, :]
        self.nc.vector.tensor_tensor(h, h, self.v["ps_u"][:, :], ALU.mult).then_inc(self.S["h_full"], 1)

    def split_hi(self, wait, j, q, reused):
        wait(self.S["h_full"], j + 1)
        if reused:
            wait(self.S["down_done"], j - 1)
        self.nc.scalar.activation(self.v["hh"][q][:, :], self.v["act_h"][q][:, :],
                                  ACT.Copy).then_inc(self.S["h_hi"], 1)

    def split_lo(self, wait, j, q, of, done="h_lo"):
        wait(self.S["h_hi"], j + 1)
        of.tensor_tensor(self.v["hl"][q][:, :], self.v["act_h"][q][:, :],
                                     self.v["hh"][q][:, :].bitcast(F32), ALU.subtract).then_inc(self.S[done], 1)

    def split_last_lo(self, wait):
        self.split_lo(wait, FJ - 1, (FJ - 1) % 2, self.nc.vector, "last_h_lo")

    def fetch_x1(self, sp, b, x1b):
        for c in range(CC):
            sp.dma_start(x1b[c][:, :], row(self.v["x1_dram"], b, c)).then_inc(self.S["x1_back"], 16)

    def store_y(self, sp, b, x1b):
        for c in range(CC):
            sp.wait_ge(self.S["down_used"], c + 1)
            sp.dma_start(row(self.v["y"], b, c), x1b[c][:, :]).then_inc(self.v["y_out"], 16)

    def add_x1(self, dve, x1b):
        dve.wait_ge(self.S["x1_back"], 16 * CC)
        for c in range(CC):
            dve.wait_ge(self.S["bank_done"], c + 1)
            self.nc.vector.tensor_tensor(x1b[c][:, :], x1b[c][:, :], self.v["ps_d"][c][:, :],
                                         ALU.add).then_inc(self.S["down_used"], 1)

    def input_hi(self, act, after_products, fresh):
        if after_products:
            act.wait_ge(self.S["up_done"], FJ)
        for c in range(CC):
            if fresh:
                act.wait_ge(self.S["base1_ready"], c + 1)
            self.nc.scalar.activation(self.v["xh"][:, c, :], self.v["base1"][:, c, :],
                                      ACT.Copy).then_inc(self.S["x_hi"], 1)

    def input_lo(self, eng, of, chunks):
        for c in chunks:
            eng.wait_ge(self.S["x_hi"], c + 1)
            of.tensor_tensor(self.v["xl"][:, c, :], self.v["base1"][:, c, :], self.v["xh"][:, c, :].bitcast(F32),
                             ALU.subtract)


def block_first(nc, v):
    sb, S, begin_round, end_round, next_round = (v[n] for n in "sb S begin_round end_round next_round".split())
    (x, k, x1_dram, rw, rb, ebh, ebl, ident, u_in, dec, osc2, base1, xh, xl) = (
        v[n] for n in "x k x1_dram rw rb ebh ebl ident u_in dec osc2 base1 xh xl".split())
    ps_a, ps_b, k_first, x_first = (v[n] for n in "ps_a ps_b k_first x_first".split())
    ps_den, ps_num, ps_mix = [v["ps_g"], v["ps_u"]], v["ps_d"][0:2], v["ps_d"][2:4]
    R2 = 2
    U = R2 * HU
    NQ = 4

    def unit(u):
        r, i = divmod(u, HU)
        return r, i, i % CC, i // CC

    def chunk_at(u):
        if u < U and unit(u)[3] == 0:
            return unit(u)[0], unit(u)[2]

    HALVED = [u for u in range(U) if unit(u)[3] == 1 or unit(u)[0] >= 1]

    MIXED = {1: (0,), 2: (1,), 3: (2,), 4: (3,)}
    BASE1 = {5: (0, 1), 6: (2, 3)}
    HIGH = {6: (0, 1), 7: (2, 3)}
    LOW = {7: (0,), 8: (1,), 9: (2,), 10: (3,)}

    def tail(table, u, behind=0):
        return [(r, c) for r in range(R2) for c in table.get(u - HU * (r + 1) + 1 - behind, ())]

    with ExitStack() as tmp:
        def t(name, shape, dt=F32):
            return sb(f"{name}_first", shape, dt, tmp)

        kb = [[t(f"kb{r}{c}", [P, T]) for c in range(CC)] for r in range(R2)]
        xb = [[t(f"xb{r}{c}", [P, T]) for c in range(CC)] for r in range(R2)]
        base0 = [t(f"base0{r}", [P, CC, T]) for r in range(R2)]
        base1_of = [t("base1", [P, CC, T]), base1]
        ek = [t(f"ek{c}", [P, T]) for c in range(CC)]
        ekv = [t(f"ekv{c}", [P, T]) for c in range(CC)]
        x1s = [*v["act_h"], *v["kb"]]
        eu, ev, fd, bd, fn, bn, den, rec, dr, quo = ([t(f"{n}{q}", [P, T]) for q in range(NQ)] for n in
                                                     "eu ev fd bd fn bn den rec dr quo".split())
        logits, marked, exps, picked = (t(n, [P, TT, E]) for n in "logits marked exps picked".split())
        ph, pl = t("picked_h", [E, T], F32R), t("picked_l", [E, T], F32R)
        eb = v["eb"] = t("eb", [E, C])
        top8 = t("top8", [P, TT, 8])
        neg_max = t("neg_max", [P, TT])
        zsum = t("zsum", [P, TT])
        zinv = t("zinv", [P, TT])
        block = tmp.enter_context(nc.Block())

        def mix_bank(r, c):
            return ps_den[c % 2] if r == R2 - 1 and c >= 2 else ps_mix[c % 2]

        def gate_base1(S, eng, of, r, c):
            eng.wait_ge(S["t1_ready"], r * CC + c + 1)
            eng.wait_ge(S["ratio_done"], (r + 1) * HU)
            of.tensor_tensor(base1_of[r][:, c, :], base0[r][:, c, :], base1_of[r][:, c, :],
                             ALU.mult).then_inc(S["base1_ready"], 1)

        @block.sync
        def _(sp):
            def load(a, dst, sems, r, c):
                sp.dma_start(dst[r][c][:, :], row(a, r, c)).then_inc(sems[r][c], 16)

            load_constants(nc, v, sp, late=False)
            load(k, kb, k_first, 0, 0)
            load(x, xb, x_first, 0, 0)
            for c in range(1, CC):
                load(k, kb, k_first, 0, c)
                load(x, xb, x_first, 0, c)
            load_constants(nc, v, sp, late=True)
            for c in range(CC):
                load(k, kb, k_first, 1, c)
                load(x, xb, x_first, 1, c)
            for s in range(2):
                sp.dma_start(v["idx_sb"][s][:, :], v["idx"][s]).then_inc(v["idx_in"][s], 16)
            for n in range(R2 * CC):
                r, c = divmod(n, CC)
                sp.wait_ge(S["x1_ready"], n + 1)
                sp.dma_start(row(x1_dram, r, c), x1s[c][:, :]).then_inc(v["x1_first"][c], 16)
            next_round(sp)

        @block.scalar
        def _(act):
            def ek_of(r, c):
                act.wait_ge(S["k_capped"], r * CC + c + 1)
                nc.scalar.activation(ek[c][:, :], ek[c][:, :], ACT.Exp).then_inc(S["ek_ready"], 1)

            def eu_of(u):
                r, i, c, layer = unit(u)
                act.wait_ge(k_first[r][c], 16)
                if u >= NQ:
                    act.wait_ge(S["den_sum"], u - NQ + 1)
                    act.wait_ge(S["lifted"], u - NQ + 1)
                n = layer * CC + c
                nc.scalar.activation(eu[u % NQ][:, :], kb[r][c][:, :], ACT.Exp,
                                     bias=u_in[:, n:n + 1]).then_inc(S["e_ready"], 1)

            def sigmoid_x(r):
                for c in range(CC):
                    act.wait_ge(x_first[r][c], 16)
                    nc.scalar.activation(base0[r][:, c, :], xb[r][c][:, :], ACT.Sigmoid).then_inc(S["t0_ready"], 1)

            def sigmoid_x1(r, c):
                act.wait_ge(S["x1_ready"], r * CC + c + 1)
                nc.scalar.activation(base0[r][:, c, :], x1s[c][:, :], ACT.Sigmoid).then_inc(S["t1_ready"], 1)

            constants_act(nc, v, act)
            ek_of(0, 0)
            eu_of(0)
            ek_of(0, 1)
            eu_of(1)
            sigmoid_x(0)
            nc.scalar.preload_act_table_set("natural_log_exp_and_others")
            for u in range(U):
                r, i, c, layer = unit(u)
                q = u % NQ
                if 1 < u + 1 < U:
                    eu_of(u + 1)
                if chunk_at(u + 2):
                    ek_of(*chunk_at(u + 2))
                for r1, c1 in tail(HIGH, u):
                    if r1 == 0:
                        act.wait_ge(S["base1_ready"], c1 + 1)
                        nc.scalar.activation(xh[:, c1, :], base1_of[0][:, c1, :], ACT.Copy).then_inc(S["x_hi"], 1)
                if u == 4:
                    act.wait_ge(v["late_consts_in"], 64)
                    nc.scalar.activation(ebh[:, :], eb[:, :], ACT.Copy).then_inc(v["eb_hi"], 1)
                    act.wait_ge(v["pool_consts"], 3)
                    nc.scalar.activation(v["ones_r"][:, :], v["ones"][0:E, :], ACT.Copy).then_inc(v["eb_hi"], 1)
                if i == 6:
                    act.wait_ge(S["top_done"], r + 1)
                    for n in range(TT):
                        ins = nc.scalar.activation(exps[:, n, :], logits[:, n, :], ACT.Exp,
                                                   bias=neg_max[:, n:n + 1], accum_out=zsum[:, n:n + 1])
                    ins.then_inc(S["exps_done"], 1)
                if i == 7:
                    act.wait_ge(S["pick_done"], r + 1)
                    nc.scalar.activation(ph[:, :], ps_b[0:E, :], ACT.Copy).then_inc(S["picked_hi"], 1)
                act.wait_ge(S["den_ready"], u + 1)
                if u >= NQ:
                    act.wait_ge(S["newton"], u - NQ + 1)
                    act.wait_ge(S["quotient"], u - NQ + 1)
                nc.scalar.activation(rec[q][:, :], den[q][:, :], ACT.Ln).then_inc(S["ln_done"], 1)
                act.wait_ge(S["ln_done"], u + 1)
                nc.scalar.activation(rec[q][:, :], rec[q][:, :], ACT.Exp, scale=-1.0).then_inc(S["recip_done"], 1)
                if i == 5 and r + 1 < R2:
                    sigmoid_x(r + 1)
                    nc.scalar.preload_act_table_set("natural_log_exp_and_others")
                if u == HU + 3:
                    for c1 in range(CC):
                        sigmoid_x1(0, c1)
                    nc.scalar.preload_act_table_set("natural_log_exp_and_others")
            for s in range(2):
                act.wait_ge(v["idx_in"][s], 16)
                narrow_idx(nc, v, s)
            for c1 in range(CC):
                sigmoid_x1(R2 - 1, c1)
            end_round(act)

        @block.gpsimd
        def _(pool):
            def refine(u):
                q = u % NQ
                pool.wait_ge(S["recip_done"], u + 1)
                if u >= NQ:
                    pool.wait_ge(S["ratio_done"], u - NQ + 1)
                nc.gpsimd.tensor_tensor(dr[q][:, :], den[q][:, :], rec[q][:, :], ALU.mult).then_inc(S["newton"], 1)

            def weigh(r, c):
                pool.wait_ge(k_first[r][c], 16)
                pool.wait_ge(S["ek_ready"], r * CC + c + 1)
                if r >= 1:
                    pool.wait_ge(S["num_scans"], 2 * (HU * (r - 1) + CC + c + 1))
                nc.gpsimd.tensor_tensor(ekv[c][:, :], ek[c][:, :], kb[r][c][:, :], ALU.mult).then_inc(S["ekv_ready"], 1)

            def gate_base0(u):
                r, i, c, layer = unit(u)
                if layer == 0:
                    pool.wait_ge(S["ratio_done"], u + 1)
                    pool.wait_ge(S["t0_ready"], r * CC + c + 1)
                    nc.gpsimd.tensor_tensor(base0[r][:, c, :], base0[r][:, c, :], quo[u % NQ][:, :],
                                            ALU.mult).then_inc(S["base0_ready"], 1)

            def lower(u):
                for r1, c1 in tail(LOW, u):
                    if r1 == 0:
                        pool.wait_ge(S["x_hi"], c1 + 1)
                        nc.gpsimd.tensor_tensor(xl[:, c1, :], base1_of[0][:, c1, :], xh[:, c1, :].bitcast(F32),
                                                ALU.subtract)

            constants_pool(nc, v, pool)
            weigh(0, 0)
            for u in range(U):
                r, i, c, layer = unit(u)
                q = u % NQ
                if u >= 1:
                    refine(u - 1)
                pool.wait_ge(S["e_capped"], u + 1)
                if u >= NQ:
                    pool.wait_ge(S["num_sum"], u - NQ + 1)
                nc.gpsimd.tensor_tensor(ev[q][:, :], eu[q][:, :], kb[r][c][:, :], ALU.mult).then_inc(S["lifted"], 1)
                if u in HALVED:
                    pool.wait_ge(S["num_scans"], 2 * (u + 1))
                    nc.gpsimd.tensor_tensor(fn[q][:, 0:T - 1], fn[q][:, 0:T - 1], bn[q][:, 0:T - 1],
                                            ALU.add).then_inc(S["num_half"], 1)
                if chunk_at(u + 1):
                    weigh(*chunk_at(u + 1))
                if u >= 1:
                    gate_base0(u - 1)
                lower(u)
                if u == 4:
                    pool.wait_ge(v["eb_hi"], 2)
                    nc.gpsimd.tensor_tensor(ebl[:, :], eb[:, :], ebh[:, :].bitcast(F32),
                                            ALU.subtract).then_inc(v["eb_lo"], 1)
            refine(U - 1)
            lower(U)
            lower(U + 1)
            for c1 in range(CC - 1):
                gate_base1(S, pool, nc.gpsimd, R2 - 1, c1)
            end_round(pool)

        @block.tensor
        def _(pe):
            def add(out, m, n, first, last):
                return nc.tensor.matmul(out[:, 0:n], ident[:, :], m[:, 0:n], start=first, stop=last)

            def total_den(u):
                q, out = u % NQ, ps_den[u % 2]
                pe.wait_ge(S["den_scans"], 2 * u + 2)
                if u >= 2:
                    pe.wait_ge(S["den_ready"], u - 1)
                add(out, fd[q], T, True, False)
                add(out, bd[q], T - 1, False, False)
                pe.wait_ge(S["e_capped"], u + 1)
                add(out, eu[q], T, False, True).then_inc(S["den_sum"], 1)

            def total_num(u):
                r, i, c, layer = unit(u)
                q, out = u % NQ, ps_num[u % 2]
                if u in HALVED:
                    pe.wait_ge(S["num_half"], HALVED.index(u) + 1)
                else:
                    pe.wait_ge(S["num_scans"], 2 * u + 2)
                if u >= 2:
                    pe.wait_ge(S["quotient"], u - 1)
                add(out, fn[q], T, True, False)
                if u not in HALVED:
                    add(out, bn[q], T - 1, False, False)
                pe.wait_ge(S["lifted"], u + 1)
                add(out, ev[q], T, False, True).then_inc(S["num_sum"], 1)

            def mix(r, c):
                n = r * CC + c
                if c == 0:
                    pe.wait_ge(v["eb_lo"], 1)
                    pe.wait_ge(S["picked_lo"], r + 1)
                    spread_picked(nc, v, ph, pl)
                if r == R2 - 1 and c >= 2:
                    pe.wait_ge(S["den_ready"], U)
                elif n >= 2:
                    pe.wait_ge(S["x1_ready"], n - 1)
                add(mix_bank(r, c), xb[r][c], T, True, False)
                mix_picked(nc, v, c, mix_bank(r, c), ph, pl, start=False)

            constants_pe(nc, v, pe)
            for u in range(U):
                r, i, c, layer = unit(u)
                if i == 7:
                    pe.wait_ge(S["picked"], r + 1)
                    for n in range(TT):
                        ins = nc.tensor.transpose(ps_b[0:E, n * P:(n + 1) * P], picked[:, n, :], ident[:, :])
                    ins.then_inc(S["pick_done"], 1)
                total_den(u)
                if i == 5:
                    pe.wait_ge(v["late_consts_in"], 64)
                    pe.wait_ge(S["base0_ready"], (r + 1) * CC)
                    for n in range(TT):
                        for c1 in range(CC):
                            ins = nc.tensor.matmul(ps_a[:, n * E:(n + 1) * E], base0[r][:, c1, n * P:(n + 1) * P],
                                                   rw[:, c1, :], start=c1 == 0, stop=c1 == CC - 1)
                    ins.then_inc(S["logits_done"], 1)
                total_num(u)
                for r1, c1 in tail(MIXED, u, -1):
                    mix(r1, c1)
            for n in range(1, CC):
                for r1, c1 in tail(MIXED, U - 1 + n, -1):
                    mix(r1, c1)
            end_round(pe)

        @block.vector
        def _(dve):
            V = nc.vector

            def cap(r, c):
                dve.wait_ge(k_first[r][c], 16)
                if r >= 1:
                    dve.wait_ge(S["den_scans"], 2 * (HU * (r - 1) + CC + c + 1))
                    dve.wait_ge(S["ekv_ready"], CC * (r - 1) + c + 1)
                V.tensor_scalar(ek[c][:, :], kb[r][c][:, :], KMAX, None, ALU.min).then_inc(S["k_capped"], 1)

            def scan_pair(src, fwd, bwd, d, done):
                V.tensor_tensor_scan(fwd[:, :], d.to_broadcast([P, T]), src[:, :], 0.0, ALU.mult,
                                     ALU.add).then_inc(done, 1)
                V.tensor_tensor_scan(bwd[:, T - 2::-1], src[:, T - 1:0:-1], d.to_broadcast([P, T - 1]), 0.0, ALU.add,
                                     ALU.mult).then_inc(done, 1)

            def guard(u):
                dve.wait_ge(S["den_sum"], u + 1)
                if u >= NQ:
                    dve.wait_ge(S["newton"], u - NQ + 1)
                V.tensor_scalar(den[u % NQ][:, :], ps_den[u % 2][:, :], DEN_MIN, None,
                                ALU.max).then_inc(S["den_ready"], 1)

            def finish(u):
                r, i, c, layer = unit(u)
                q = u % NQ
                dve.wait_ge(S["num_sum"], u + 1)
                dve.wait_ge(S["recip_done"], u + 1)
                if u >= NQ and unit(u - NQ)[3] == 0:
                    dve.wait_ge(S["base0_ready"], unit(u - NQ)[0] * CC + unit(u - NQ)[2] + 1)
                V.scalar_tensor_tensor(out=quo[q][:, :], in0=ps_num[u % 2][:, :], scalar=osc2[:, r:r + 1],
                                       in1=rec[q][:, :], op0=ALU.mult, op1=ALU.mult).then_inc(S["quotient"], 1)
                dve.wait_ge(S["quotient"], u + 1)
                dve.wait_ge(S["newton"], u + 1)
                dst = (quo[q][:, :], base1_of[r][:, c, :])[layer]
                V.scalar_tensor_tensor(out=dst, in0=dr[q][:, :], scalar=2.0, in1=quo[q][:, :], op0=ALU.subtract,
                                       op1=ALU.mult).then_inc(S["ratio_done"], 1)

            def weigh_base0(r, c):
                dve.wait_ge(S["spread_done"], r + 1)
                V.tensor_tensor(base0[r][:, c, :], base0[r][:, c, :], ps_a[:, :], ALU.mult).then_inc(S["mix_half"], 1)

            def residual(r, c):
                n = r * CC + c
                dve.wait_ge(S["mix_half"], n + 1)
                dve.wait_ge(S["mix_done"], n + 1)
                if r >= 1:
                    dve.wait_ge(v["x1_first"][c], 16 * r)
                V.tensor_tensor(x1s[c][:, :], base0[r][:, c, :], mix_bank(r, c)[:, :],
                                ALU.add).then_inc(S["x1_ready"], 1)

            chain = [0]

            def link(ins):
                chain[0] += 1
                ins.then_inc(S["l0_chain"], 1)

            def linked():
                dve.wait_ge(S["l0_chain"], chain[0])

            def find_top():
                dve.wait_ge(S["logits_done"], r + 1)
                dve.wait_ge(v["late_consts_in"], 64)
                link(V.tensor_tensor(logits[:, :, :], ps_a[:, 0:TT * E].rearrange("p (t e) -> p t e", e=E),
                                     rb[:, None, :].to_broadcast([P, TT, E]), ALU.add))
                linked()
                for n in range(TT):
                    link(V.max(top8[:, n, :], logits[:, n, :]))
                linked()
                V.tensor_scalar(neg_max[:, :], top8[:, :, 0], -1.0, None, ALU.mult).then_inc(S["top_done"], 1)
                for n in range(TT):
                    link(V.match_replace(marked[:, n, :], top8[:, n, :], logits[:, n, :], TAKEN))
                linked()
                link(V.tensor_tensor(marked[:, :, :], marked[:, :, :], logits[:, :, :], ALU.not_equal))

            def weigh_top():
                dve.wait_ge(S["exps_done"], r + 1)
                link(V.reciprocal(zinv[:, :], zsum[:, :]))
                linked()
                link(V.tensor_tensor(picked[:, :, :], marked[:, :, :], exps[:, :, :], ALU.mult))
                linked()
                V.tensor_tensor(picked[:, :, :], picked[:, :, :], zinv[:, :, None].to_broadcast([P, TT, E]),
                                ALU.mult).then_inc(S["picked"], 1)

            cap(0, 0)
            cap(0, 1)
            constants_dve(nc, v, dve, late=False)
            for u in range(U):
                r, i, c, layer = unit(u)
                q = u % NQ
                d = dec[:, r, layer * CC + c:layer * CC + c + 1]
                dve.wait_ge(S["ek_ready"], r * CC + c + 1)
                if u >= NQ:
                    dve.wait_ge(S["den_sum"], u - NQ + 1)
                scan_pair(ek[c], fd[q], bd[q], d, S["den_scans"])
                dve.wait_ge(S["e_ready"], u + 1)
                V.tensor_scalar(eu[q][:, :], eu[q][:, :], EXP_KMAX, None, ALU.min).then_inc(S["e_capped"], 1)
                dve.wait_ge(S["ekv_ready"], r * CC + c + 1)
                if u >= NQ:
                    dve.wait_ge(S["num_sum"], u - NQ + 1)
                scan_pair(ekv[c], fn[q], bn[q], d, S["num_scans"])
                if u == 0:
                    constants_dve(nc, v, dve, late=True)
                if i == 6:
                    find_top()
                if chunk_at(u + 2):
                    cap(*chunk_at(u + 2))
                if u >= 1:
                    finish(u - 1)
                guard(u)
                if i == 6:
                    weigh_top()
                if i == 7:
                    lower_picked(nc, v, dve, r + 1, ph, pl)
                for r1, c1 in tail(MIXED, u):
                    weigh_base0(r1, c1)
                    residual(r1, c1)
                for r1, c1 in tail(BASE1, u):
                    gate_base1(S, dve, V, r1, c1)
            finish(U - 1)
            constants_lut(nc, v, dve)
            dve.wait_ge(v["idx_narrow"], 1)
            take_bits03(V, v, 0)
            for c1 in range(CC + 1):
                if c1 < CC:
                    weigh_base0(R2 - 1, c1)
                if c1 >= 1:
                    residual(R2 - 1, c1 - 1)
            gate_base1(S, dve, V, R2 - 1, CC - 1)
            end_round(dve)


def take_bits03(V, v, p):
    V.tensor_scalar(v["bits03"][p], v["idx16"][p], 5, 0x100 + BIT0, ALU.logical_shift_left,
                    ALU.bitwise_and).then_inc(v["bits03_ready"], 1)


def narrow_idx(nc, v, p):
    nc.scalar.activation(v["idx16"][p], v["idx_sb"][p][:, :], ACT.Copy).then_inc(v["idx_narrow"], 1)


def block_lookup(nc, v):
    sb = v["sb"]
    (idx, wh, wl, lut_in, lut_d, hold) = (v[n] for n in "idx wh wl lut_in lut_d hold".split())
    (idx_in, idx_narrow, bits03_ready, bits12_ready, leaves_act, leaves_pool, pairs_done, fours_done, weight_full,
     weight_hi, weight_lo) = (v[n] for n in ("idx_in idx_narrow bits03_ready bits12_ready leaves_act leaves_pool "
                                             "pairs_done fours_done weight_full weight_hi weight_lo").split())
    begin_round, end_round, next_round = v["begin_round"], v["end_round"], v["next_round"]
    prod = Products(nc, v)
    ROUND = 1
    ACT_LEAVES = ((2, 4, 1, 0), (2, 4, 1, 0), (2, 4, 6, 1, 0))
    POOL_LEAVES = ((3, 5, 6, 7), (3, 5, 6, 7), (3, 5, 7))
    with ExitStack() as tmp:
        idx_sb, idx16, bits03 = v["idx_sb"], v["idx16"], v["bits03"]
        bits12 = [sb(f"bits12_{p}", [P, SB], I16, tmp) for p in range(2)]
        odd = [sb(f"leaf_{n}", [P, SB], F32, tmp) for n in (1, 3, 5, 7)]
        even = [[sb(f"leaf{p}_{n}", [P, SB], F32, tmp) for n in (0, 2, 4, 6)] for p in range(2)]
        x1b = [sb(f"x1b{c}", [P, T], F32, tmp) for c in range(CC)]

        def leaf(p, n):
            return odd[n // 2] if n % 2 else even[p][n // 2]

        def bit(p, n):
            pair = (bits12[p][:, :] if n in (1, 2) else bits03[p]).bitcast(U8).rearrange("p (n two) -> p n two", two=2)
            return pair[:, :, n // 2]

        wh_flat = wh[:, :, :].rearrange("p j n -> p (j n)")
        wl_flat = wl[:, :, :].rearrange("p j n -> p (j n)")
        idx_flat = idx.rearrange("s p n -> (s p) n")
        block = tmp.enter_context(nc.Block())

        def chunks(eng, step):
            def chunk(j, q):
                for part in range(3):
                    step(3 * j + part, (3 * q + part) % 2, j, q, part)
            for j in range(3):
                chunk(j, j % 2)
            with eng.Fori(0, (FJ - 3) // 2) as it:
                for jj in range(2):
                    chunk(2 * it + (3 + jj), 1 - jj)

        def at_least(j, n):
            return not isinstance(j, int) or j >= n

        @block.sync
        def _(sp):
            begin_round(sp, "sp", ROUND)
            for c in range(CC):
                sp.wait_ge(v["x1_first"][c], 32)

            def step(s, p, j, q, part):
                if isinstance(s, int) and s == 6:
                    prod.fetch_x1(sp, 0, x1b)
                    load_k_ahead(v, sp, 2)
                sp.wait_ge(idx_narrow, s + 1)
                sp.dma_start(idx_sb[p][:, :], idx_flat[bass.ds((s + 2) * P, P), :]).then_inc(idx_in[p], 16)

            chunks(sp, step)
            sp.wait_ge(idx_in[0], 16 * ((NS + 3) // 2))
            sp.wait_ge(idx_in[1], 16 * ((NS + 2) // 2))
            prod.store_y(sp, 0, x1b)
            sp.wait_ge(v["S"]["k_ahead"], 32)
            next_round(sp)

        def leaves(wait, of, s, p, which, done, each):
            wait(bits03_ready, s + 1)
            for n in which:
                sm, count = ((pairs_done, 4 * s - 4 + (n + 1) // 2) if n % 2 else
                             (weight_full, s - 1) if n else (weight_lo, s - 1))
                if not isinstance(count, int) or (count > 0 and s > 0):
                    wait(sm, count)
                args = (leaf(p, n)[:, :], bit(p, 0))
                if of is nc.scalar:
                    ins = of.activation(*args, ACT.Identity, bias=lut_in[:, 2 * n:2 * n + 1],
                                        scale=lut_d[:, n:n + 1])
                else:
                    ins = of.tensor_scalar(*args, lut_d[:, n:n + 1], lut_in[:, 2 * n:2 * n + 1], ALU.mult, ALU.add)
                if each or n == which[-1]:
                    ins.then_inc(done, 1)

        @block.scalar
        def _(act):
            def wait(sm, val):
                hold(act, "act", sm, val)

            def narrow(s, p):
                wait(idx_in[p], 8 * (s - p) + 16)
                narrow_idx(nc, v, p)

            begin_round(act, "act", ROUND)
            leaves(wait, nc.scalar, 0, 0, ACT_LEAVES[0], leaves_act, False)

            def step(s, p, j, q, part):
                leaves(wait, nc.scalar, s + 1, 1 - p, ACT_LEAVES[(part + 1) % 3], leaves_act, False)
                if isinstance(s, int) and s == 2:
                    nc.scalar.preload_act_table_set("silu_and_others")
                if part == 2:
                    prod.silu(wait, j, q, at_least(j, 2))
                if part == 0 and at_least(j, 1):
                    prod.split_hi(wait, j - 1, 1 - q, at_least(j, 3))
                wait(bits12_ready, s + 1)
                narrow(s + 2, p)
                wait(weight_full, s + 1)
                nc.scalar.activation(wh_flat[:, bass.ds(s * SB, SB)], leaf(p, 0)[:, :],
                                     ACT.Copy).then_inc(weight_hi, 1)

            chunks(act, step)
            prod.split_hi(wait, FJ - 1, (FJ - 1) % 2, True)
            prod.input_hi(act, True, fresh=False)
            end_round(act)

        @block.gpsimd
        def _(pool):
            def wait(sm, val):
                hold(pool, "pool", sm, val)

            begin_round(pool, "pool", ROUND)
            leaves(wait, nc.gpsimd, 0, 0, POOL_LEAVES[0], leaves_pool, True)

            def step(s, p, j, q, part):
                leaves(wait, nc.gpsimd, s + 1, 1 - p, POOL_LEAVES[(part + 1) % 3], leaves_pool, True)
                if part == 1 and at_least(j, 1):
                    prod.split_lo(wait, j - 1, 1 - q, nc.gpsimd)
                wait(weight_hi, s + 1)
                nc.gpsimd.tensor_tensor(wl_flat[:, bass.ds(s * SB, SB)], leaf(p, 0)[:, :],
                                        wh_flat[:, bass.ds(s * SB, SB)].bitcast(F32),
                                        ALU.subtract).then_inc(weight_lo, 1)

            chunks(pool, step)
            prod.input_lo(pool, nc.gpsimd, (0, 2, 3))
            end_round(pool)

        @block.tensor
        def _(pe):
            begin_round(pe, "pe", ROUND)
            for j in range(FJ):
                pe.wait_ge(weight_lo, 3 * j + 1)
                prod.gate(pe, j)
                pe.wait_ge(weight_lo, 3 * j + 2)
                prod.up(pe, j)
                if j >= 1:
                    prod.down(pe, j - 1)
            pe.wait_ge(weight_lo, 3 * FJ)
            prod.down(pe, FJ - 1)
            end_round(pe)

        @block.vector
        def _(dve):
            V = nc.vector

            def wait(sm, val):
                hold(dve, "dve", sm, val)

            def select(p, a, n):
                return V.copy_predicated(leaf(p, a)[:, :], bit(p, n), leaf(p, a + (1 << (n - 1)))[:, :])

            def take_bits12(s, p):
                V.tensor_scalar(bits12[p][:, :], idx16[p], 6, 0x180, ALU.logical_shift_left,
                                ALU.bitwise_and).then_inc(bits12_ready, 1)

            begin_round(dve, "dve", ROUND)
            take_bits12(0, 0)

            def step(s, p, j, q, part):
                wait(bits12_ready, s + 1)
                wait(leaves_act, s + 1)
                select(p, 0, 1).then_inc(pairs_done, 1)
                wait(idx_narrow, s + 2)
                if at_least(s, 1):
                    wait(weight_full, s)
                take_bits03(V, v, 1 - p)
                of_pool = [sum(map(len, POOL_LEAVES[:m])) for m in range(4)]
                for a in (2, 4, 6):
                    wait(leaves_pool, j * of_pool[3] + of_pool[part] + POOL_LEAVES[part].index(a + 1) + 1)
                    select(p, a, 1).then_inc(pairs_done, 1)
                wait(pairs_done, 4 * s + 2)
                select(p, 0, 2).then_inc(fours_done, 1)
                if part == 0 and at_least(j, 1):
                    prod.hidden(wait, j - 1, 1 - q)
                wait(pairs_done, 4 * s + 4)
                select(p, 4, 2).then_inc(fours_done, 1)
                take_bits12(s + 1, 1 - p)
                wait(fours_done, 2 * s + 2)
                select(p, 0, 3).then_inc(weight_full, 1)

            chunks(dve, step)
            prod.hidden(wait, FJ - 1, (FJ - 1) % 2)
            prod.split_last_lo(wait)
            prod.input_lo(dve, V, (1,))
            prod.add_x1(dve, x1b)
            end_round(dve)


def block_rounds(nc, v, rounds):
    sb, S, hold = v["sb"], v["S"], v["hold"]
    begin_round, end_round, next_round = v["begin_round"], v["end_round"], v["next_round"]
    (x, k, x1_dram, rw, rb, ident, u_in, dec, osc, base1) = (
        v[n] for n in "x k x1_dram rw rb ident u_in dec osc base1".split())
    ps_a, ps_b, y_out = v["ps_a"], v["ps_b"], v["y_out"]
    prod = Products(nc, v)
    with ExitStack() as tmp:
        def t(name, shape, dt=F32):
            return sb(f"{name}_rounds", shape, dt, tmp)

        dec_cur, osc_cur, kb = v["dec_cur"], v["osc_cur"], v["kb"]
        base0 = t("base0", [P, CC, T])
        ek = [t(f"ek{p}", [P, T]) for p in range(2)]
        ekv = [t(f"ekv{p}", [P, T]) for p in range(2)]
        eu = [v["idx_parts"][:, p, :, :].rearrange("p a n -> p (a n)").bitcast(F32) for p in range(2)]
        fd = [v["idx_sb"][p][:, :].bitcast(F32) for p in range(2)]
        bd = [t(f"bd{p}", [P, T]) for p in range(2)]
        fn = [t(f"fn{p}", [P, T]) for p in range(2)]
        bn = [t(f"bn{p}", [P, T]) for p in range(2)]
        xs = ek
        ph, pl = t("picked_h", [E, T], F32R), t("picked_l", [E, T], F32R)
        top8 = t("top8", [P, TT, 8])
        neg_max = t("neg_max", [P, TT])
        zsum = t("zsum", [P, TT])
        zinv = t("zinv", [P, TT])
        logits = fd[0][:, 0:TT * E].rearrange("p (t e) -> p t e", e=E)
        marked = fd[0][:, TT * E:2 * TT * E].rearrange("p (t e) -> p t e", e=E)
        exps = bd[0][:, 0:TT * E].rearrange("p (t e) -> p t e", e=E)
        picked = bd[0][:, TT * E:2 * TT * E].rearrange("p (t e) -> p t e", e=E)
        x1b = [fd[1], bd[1], fn[1], bn[1]]

        block = tmp.enter_context(nc.Block())

        def run(eng, body):
            for number, g, r in rounds:
                if number == "loop":
                    first, count = g, r
                    with eng.Fori(0, count) as it:
                        body(it + first, it + (first - 1), it + first)
                else:
                    body(number, g, r)

        @block.sync
        def _(sp):
            def store_x1(r, c):
                sp.wait_ge(S["x1_ready"], c + 1)
                sp.dma_start(row(x1_dram, r, c), xs[c % 2][:, :]).then_inc(S[f"x1_out{c % 2}"], 16)

            def body(number, g, r):
                begin_round(sp, "sp", number)
                if r is not None:
                    for c in range(CC):
                        sp.dma_start(base0[:, c, :], row(x, r, c)).then_inc(S[f"x_in{c}"], 16)
                if r is not None:
                    for c in range(2, CC):
                        sp.wait_ge(S["lifted"], 2 * (c - 1))
                        sp.wait_ge(S["ekv_ready"], c - 1)
                        sp.dma_start(kb[c % 2][:, :], row(k, r, c)).then_inc(S[f"k_in{c % 2}"], 16)
                    sp.wait_ge(S["ratio_done"], HU)
                    for c in range(2):
                        sp.dma_start(xs[c][:, :], row(x, r, c)).then_inc(S[f"xb_in{c}"], 16)
                    prod.fetch_x1(sp, g, x1b)
                    load_k_ahead(v, sp, r + 1)
                    for c in range(CC):
                        if c >= 2:
                            sp.wait_ge(S[f"x1_out{c % 2}"], 16)
                            sp.wait_ge(S["t1_ready"], c - 1)
                            sp.dma_start(xs[c % 2][:, :], row(x, r, c)).then_inc(S[f"xb_in{c % 2}"], 16)
                        if c >= 1:
                            store_x1(r, c - 1)
                    store_x1(r, CC - 1)
                if r is None:
                    prod.fetch_x1(sp, g, x1b)
                prod.store_y(sp, g, x1b)
                if r is not None:
                    sp.wait_ge(S["k_ahead"], 32)
                    sp.wait_ge(S["x1_out0"], 32)
                    sp.wait_ge(S["x1_out1"], 32)
                next_round(sp)

            run(sp, body)
            sp.wait_ge(y_out, 16 * B * CC)

        @block.scalar
        def _(act):
            def ek_of(c):
                act.wait_ge(S["k_capped"], c + 1)
                nc.scalar.activation(ek[c % 2][:, :], ek[c % 2][:, :], ACT.Exp).then_inc(S["ek_ready"], 1)

            def eu_of(i):
                c, layer = divmod(i, 2)
                if layer == 0 and c >= 2:
                    act.wait_ge(S[f"k_in{c % 2}"], 16)
                if i >= 2:
                    act.wait_ge(S["num_full"], i - 1)
                n = layer * CC + c
                nc.scalar.activation(eu[i % 2][:, :], kb[c % 2][:, :], ACT.Exp,
                                     bias=u_in[:, n:n + 1]).then_inc(S["e_ready"], 1)

            def tanh_x(c):
                act.wait_ge(S[f"x_in{c}"], 16)
                nc.scalar.activation(base0[:, c, :], base0[:, c, :], ACT.Tanh, scale=0.5).then_inc(S["t0_ready"], 1)

            def body(number, g, r):
                G, R = g is not None, r is not None
                begin_round(act, "act", number)
                if R:
                    nc.scalar.preload_act_table_set("natural_log_exp_and_others")
                    ek_of(0)
                    eu_of(0)
                    eu_of(1)
                for j in range(FJ + 1):
                    rec = R and j < HU
                    if G and j >= 1:
                        prod.split_hi(act.wait_ge, j - 1, (j - 1) % 2, j >= 3)
                    if rec and 0 < j < HU - 1:
                        eu_of(j + 1)
                        if j % 2 == 1:
                            ek_of(j // 2 + 1)
                    if R and j == 8:
                        act.wait_ge(S["top_done"], 1)
                        for n in range(TT):
                            ins = nc.scalar.activation(exps[:, n, :], logits[:, n, :], ACT.Exp,
                                                       bias=neg_max[:, n:n + 1], accum_out=zsum[:, n:n + 1])
                        ins.then_inc(S["exps_done"], 1)
                    if R and j == 9:
                        act.wait_ge(S["pick_done"], 1)
                        nc.scalar.activation(ph[:, :], ps_b[0:E, :], ACT.Copy).then_inc(S["picked_hi"], 1)
                    if G and j < FJ:
                        prod.silu(act.wait_ge, j, j % 2, j >= 2)
                    if G and R and j < CC:
                        tanh_x(j)
                    if R and j in (9, 10, 11):
                        for c1 in {9: (0, 1), 10: (2, 3), 11: ()}[j]:
                            act.wait_ge(S["x1_ready"], c1 + 1)
                            nc.scalar.activation(base0[:, c1, :], xs[c1 % 2][:, :], ACT.Tanh,
                                                 scale=0.5).then_inc(S["t1_ready"], 1)
                    if rec:
                        if G:
                            nc.scalar.preload_act_table_set("natural_log_exp_and_others")
                        act.wait_ge(S["den_ready"], j + 1)
                        nc.scalar.activation(fd[j % 2][:, :], bd[j % 2][:, :], ACT.Ln).then_inc(S["ln_done"], 1)
                        act.wait_ge(S["ln_done"], j + 1)
                        nc.scalar.activation(fd[j % 2][:, :], fd[j % 2][:, :], ACT.Exp,
                                             scale=-1.0).then_inc(S["recip_done"], 1)
                if R:
                    prod.input_hi(act, True, fresh=True)
                end_round(act)

            run(act, body)

        @block.gpsimd
        def _(pool):
            def refine(i):
                pool.wait_ge(S["recip_done"], i + 1)
                nc.gpsimd.tensor_tensor(bd[i % 2][:, :], bd[i % 2][:, :], fd[i % 2][:, :],
                                        ALU.mult).then_inc(S["newton"], 1)

            def weigh(c):
                pool.wait_ge(S["ek_ready"], c + 1)
                if c >= 2:
                    pool.wait_ge(S["num_scans"], 4 * (c - 1))
                nc.gpsimd.tensor_tensor(ekv[c % 2][:, :], ek[c % 2][:, :], kb[c % 2][:, :],
                                        ALU.mult).then_inc(S["ekv_ready"], 1)

            def body(number, g, r):
                G, R = g is not None, r is not None
                begin_round(pool, "pool", number)
                if R:
                    weigh(0)
                for j in range(FJ + 1):
                    c, layer = divmod(j, 2)
                    q = j % 2
                    rec = R and j < HU
                    if G and 1 <= j < FJ:
                        prod.split_lo(pool.wait_ge, j - 1, (j - 1) % 2, nc.gpsimd)
                    if rec:
                        pool.wait_ge(S["den_part"], j + 1)
                        nc.gpsimd.tensor_tensor(fd[q][:, 0:T - 1], fd[q][:, 0:T - 1], bd[q][:, 0:T - 1],
                                                ALU.add).then_inc(S["den_sum"], 1)
                    if R and 1 <= j <= HU:
                        refine(j - 1)
                    if rec:
                        pool.wait_ge(S["num_scans"], 2 * (j + 1))
                        nc.gpsimd.tensor_tensor(fn[q][:, 0:T - 1], fn[q][:, 0:T - 1], bn[q][:, 0:T - 1],
                                                ALU.add).then_inc(S["num_sum"], 1)
                        pool.wait_ge(S["num_sum"], j + 1)
                        pool.wait_ge(S["lifted"], j + 1)
                        nc.gpsimd.tensor_tensor(fn[q][:, :], fn[q][:, :], eu[q][:, :],
                                                ALU.add).then_inc(S["num_full"], 1)
                        if layer == 1 and c + 1 < CC:
                            weigh(c + 1)
                    if R and j in (9, 10, 11):
                        for c1 in {9: (0, 1), 10: (2, 3), 11: ()}[j]:
                            pool.wait_ge(S["mixed"], c1 + 1)
                            pool.wait_ge(S[f"xb_in{c1 % 2}"], 16 * (c1 // 2 + 1))
                            nc.gpsimd.tensor_tensor(xs[c1 % 2][:, :], base0[:, c1, :], xs[c1 % 2][:, :],
                                                    ALU.add).then_inc(S["x1_ready"], 1)
                if R:
                    prod.input_lo(pool, nc.gpsimd, (0, 2, 3))
                end_round(pool)

            run(pool, body)

        @block.tensor
        def _(pe):
            def mix(c):
                if c >= 1:
                    pe.wait_ge(S["mixed"], c)
                mix_picked(nc, v, c, ps_b, ph, pl, start=True)

            def body(number, g, r):
                G, R = g is not None, r is not None
                begin_round(pe, "pe", number)
                for j in range(FJ):
                    if R and j == 9:
                        pe.wait_ge(S["picked_lo"], 1)
                        spread_picked(nc, v, ph, pl)
                        mix(0)
                    if R and j == 10:
                        mix(2)
                    if G:
                        prod.gate(pe, j)
                    if R and j == 9:
                        mix(1)
                    if R and j == 10:
                        mix(3)
                    if G:
                        prod.up(pe, j)
                    if R and j == 7:
                        pe.wait_ge(S["base0_ready"], CC)
                        for n in range(TT):
                            for c in range(CC):
                                ins = nc.tensor.matmul(ps_a[:, n * E:(n + 1) * E], base0[:, c, n * P:(n + 1) * P],
                                                       rw[:, c, :], start=c == 0, stop=c == CC - 1)
                        ins.then_inc(S["logits_done"], 1)
                    if R and j == 8:
                        pe.wait_ge(S["picked"], 1)
                        for n in range(TT):
                            ins = nc.tensor.transpose(ps_b[0:E, n * P:(n + 1) * P], picked[:, n, :], ident[:, :])
                        ins.then_inc(S["pick_done"], 1)
                    if G and j >= 1:
                        prod.down(pe, j - 1)
                if G:
                    prod.down(pe, FJ - 1)
                end_round(pe)

            run(pe, body)

        @block.vector
        def _(dve):
            V = nc.vector

            def cap(c):
                if c >= 2:
                    dve.wait_ge(S[f"k_in{c % 2}"], 16)
                    dve.wait_ge(S["ekv_ready"], c - 1)
                V.tensor_scalar(ek[c % 2][:, :], kb[c % 2][:, :], KMAX, None, ALU.min).then_inc(S["k_capped"], 1)

            def scan_pair(src, fwd, bwd, d, done):
                V.tensor_tensor_scan(fwd[:, :], d.to_broadcast([P, T]), src[:, :], 0.0, ALU.mult,
                                     ALU.add).then_inc(done, 1)
                V.tensor_tensor_scan(bwd[:, T - 2::-1], src[:, T - 1:0:-1], d.to_broadcast([P, T - 1]), 0.0, ALU.add,
                                     ALU.mult).then_inc(done, 1)

            def finish(i):
                c, layer = divmod(i, 2)
                q = i % 2
                dve.wait_ge(S["num_full"], i + 1)
                dve.wait_ge(S["recip_done"], i + 1)
                V.scalar_tensor_tensor(out=fn[q][:, :], in0=fn[q][:, :], scalar=osc_cur[:, 0:1], in1=fd[q][:, :],
                                       op0=ALU.mult, op1=ALU.mult).then_inc(S["quotient"], 1)
                dve.wait_ge(S["quotient"], i + 1)
                dve.wait_ge(S["newton"], i + 1)
                dst = (fn[q][:, :], base1[:, c, :])[layer]
                V.scalar_tensor_tensor(out=dst, in0=bd[q][:, :], scalar=2.0, in1=fn[q][:, :], op0=ALU.subtract,
                                       op1=ALU.mult).then_inc(S["ratio_done"], 1)
                if layer == 0:
                    dve.wait_ge(S["ratio_done"], i + 1)
                    dve.wait_ge(S["t0_ready"], c + 1)
                    V.scalar_tensor_tensor(out=base0[:, c, :], in0=base0[:, c, :], scalar=1.0, in1=dst, op0=ALU.add,
                                           op1=ALU.mult).then_inc(S["base0_ready"], 1)

            def recurrence(j, G, g):
                c, layer = divmod(j, 2)
                q = j % 2
                d = dec_cur[:, layer * CC + c:layer * CC + c + 1]
                if j >= 2:
                    dve.wait_ge(S["ratio_done"], j - 1)
                    dve.wait_ge(S["base0_ready"], (j - 1 + 1) // 2)
                dve.wait_ge(S["ek_ready"], c + 1)
                scan_pair(ek[c % 2], fd[q], bd[q], d, S["den_scans"])
                dve.wait_ge(S["den_scans"], 2 * j + 2)
                dve.wait_ge(S["e_ready"], j + 1)
                V.scalar_tensor_tensor(out=fd[q][:, :], in0=eu[q][:, :], scalar=EXP_KMAX, in1=fd[q][:, :],
                                       op0=ALU.min, op1=ALU.add).then_inc(S["den_part"], 1)
                V.scalar_tensor_tensor(out=eu[q][:, :], in0=eu[q][:, :], scalar=EXP_KMAX, in1=kb[c % 2][:, :],
                                       op0=ALU.min, op1=ALU.mult).then_inc(S["lifted"], 1)
                if j == 0:
                    hold(dve, "dve", y_out, 16 * CC * g)
                dve.wait_ge(S["ekv_ready"], c + 1)
                scan_pair(ekv[c % 2], fn[q], bn[q], d, S["num_scans"])
                if j >= 1:
                    finish(j - 1)
                dve.wait_ge(S["den_sum"], j + 1)
                V.tensor_scalar(bd[q][:, :], fd[q][:, :], DEN_MIN, None, ALU.max).then_inc(S["den_ready"], 1)
                if layer == 0 and c + 1 < CC:
                    cap(c + 1)

            def body(number, g, r):
                G, R = g is not None, r is not None
                begin_round(dve, "dve", number)
                if R:
                    V.tensor_copy(dec_cur[:, :], dec[:, bass.ds(r, 1), :].rearrange("p b n -> p (b n)")
                                  ).then_inc(S["cur_ready"], 1)
                    V.tensor_copy(osc_cur[:, :], osc[:, bass.ds(r, 1)]).then_inc(S["cur_ready"], 1)
                    cap(0)
                    dve.wait_ge(S["cur_ready"], 2)
                for j in range(FJ + 1):
                    if G and j >= 1:
                        prod.hidden(dve.wait_ge, j - 1, (j - 1) % 2)
                    if G and j == FJ:
                        prod.split_last_lo(dve.wait_ge)
                    if R and j < HU:
                        recurrence(j, G, g)
                    if R and j == HU:
                        finish(HU - 1)
                        top_k()
                    if R and j == 9:
                        lower_picked(nc, v, dve, 1, ph, pl)
                    if R and j in (9, 10, 11):
                        for c1 in {9: (0, 1), 10: (2, 3), 11: ()}[j]:
                            mixture(c1)
                        for c1 in {9: (), 10: (0, 1, 2), 11: (3,)}[j]:
                            dve.wait_ge(S["t1_ready"], c1 + 1)
                            V.scalar_tensor_tensor(out=base1[:, c1, :], in0=base0[:, c1, :], scalar=1.0,
                                                   in1=base1[:, c1, :], op0=ALU.add,
                                                   op1=ALU.mult).then_inc(S["base1_ready"], 1)
                if R:
                    prod.input_lo(dve, V, (1,))
                if G:
                    prod.add_x1(dve, x1b)
                end_round(dve)

            def top_k():
                chain = [0]

                def link(ins):
                    chain[0] += 1
                    ins.then_inc(S["l0_chain"], 1)

                def linked():
                    dve.wait_ge(S["l0_chain"], chain[0])

                dve.wait_ge(S["logits_done"], 1)
                dve.wait_ge(S["ratio_done"], HU)
                link(V.tensor_tensor(logits, ps_a[:, 0:TT * E].rearrange("p (t e) -> p t e", e=E),
                                     rb[:, None, :].to_broadcast([P, TT, E]), ALU.add))
                linked()
                for n in range(TT):
                    link(V.max(top8[:, n, :], logits[:, n, :]))
                linked()
                V.tensor_scalar(neg_max[:, :], top8[:, :, 0], -1.0, None, ALU.mult).then_inc(S["top_done"], 1)
                for n in range(TT):
                    link(V.match_replace(marked[:, n, :], top8[:, n, :], logits[:, n, :], TAKEN))
                linked()
                link(V.tensor_tensor(marked, marked, logits, ALU.not_equal))
                dve.wait_ge(S["exps_done"], 1)
                link(V.reciprocal(zinv[:, :], zsum[:, :]))
                linked()
                link(V.tensor_tensor(picked, marked, exps, ALU.mult))
                linked()
                V.tensor_tensor(picked, picked, zinv[:, :, None].to_broadcast([P, TT, E]),
                                ALU.mult).then_inc(S["picked"], 1)

            def mixture(c):
                if c == 0:
                    dve.wait_ge(S["spread_done"], 1)
                V.tensor_tensor(base0[:, c, :], base0[:, c, :], ps_a[:, :], ALU.mult).then_inc(S["mix_half"], 1)
                dve.wait_ge(S["mix_half"], c + 1)
                dve.wait_ge(S["mix_done"], c + 1)
                V.tensor_tensor(base0[:, c, :], base0[:, c, :], ps_b[:, :], ALU.add).then_inc(S["mixed"], 1)

            run(dve, body)


def lower_picked(nc, v, dve, count, ph, pl):
    dve.wait_ge(v["S"]["picked_hi"], count)
    nc.vector.tensor_tensor(pl[:, :], v["ps_b"][0:E, :], ph[:, :].bitcast(F32),
                            ALU.subtract).then_inc(v["S"]["picked_lo"], 1)


def spread_picked(nc, v, ph, pl):
    out, ones_r = v["ps_a"][:, :], v["ones_r"][:, :]
    nc.tensor.matmul(out, ones_r, ph[:, :], start=True, stop=False)
    nc.tensor.matmul(out, ones_r, pl[:, :], start=False, stop=True).then_inc(v["S"]["spread_done"], 1)


def mix_picked(nc, v, c, out, ph, pl, start):
    h, l = (v[n][:, c * P:(c + 1) * P] for n in ("ebh", "ebl"))
    nc.tensor.matmul(out[:, :], h, ph[:, :], start=start, stop=False)
    nc.tensor.matmul(out[:, :], l, ph[:, :], start=False, stop=False)
    nc.tensor.matmul(out[:, :], h, pl[:, :], start=False, stop=True).then_inc(v["S"]["mix_done"], 1)


def load_k_ahead(v, sp, r):
    for c in range(2):
        sp.dma_start(v["kb"][c][:, :], row(v["k"], r, c)).then_inc(v["S"]["k_ahead"], 16)


def load_constants(nc, v, sp, late):
    small = {"cond": v["cond_t"], "w": v["w_in"], "u": v["u_in"]}
    big = {"lut": v["lut_in"], "router_b": v["rb"], "expert_b": v["eb"], "router_w": v["rw"]}
    for n, dst in (big if late else small).items():
        src = v[n]
        if n in ("lut", "router_b"):
            src = src.to_broadcast([P, src.shape[1]])
        if n == "router_w":
            sp.dma_start(dst[:, :, :], src).then_inc(v["late_consts_in"], 16)
        elif late:
            sp.dma_start(dst[:, :], src).then_inc(v["late_consts_in"], 16)
        else:
            sp.dma_start(dst[:, :], src).then_inc(v["consts_in"], 16)


def constants_act(nc, v, act):
    tf, dec0, ps_a, w_in, setup_exp = (v[n] for n in "tf dec0 ps_a w_in setup_exp".split())
    nc.scalar.preload_act_table_set("natural_log_exp_and_others")
    act.wait_ge(v["consts_in"], 48)
    act.wait_ge(v["cond_sum"], 1)
    nc.scalar.activation(tf[:, 0, :], ps_a[:, 0:B], ACT.Exp, scale=-1.0).then_inc(setup_exp, 1)
    nc.scalar.activation(dec0[:, 0, :], w_in[:, :], ACT.Exp).then_inc(setup_exp, 1)
    act.wait_ge(setup_exp, 2)
    nc.scalar.activation(dec0[:, 1, :], dec0[:, 0, :], ACT.Exp, scale=-1.0).then_inc(setup_exp, 1)


def constants_pool(nc, v, pool):
    ones, ident, pool_consts = (v[n] for n in "ones ident pool_consts".split())
    nc.gpsimd.memset(ones[:, :], 1.0).then_inc(pool_consts, 1)
    nc.gpsimd.memset(ident[:, :], 0.0).then_inc(pool_consts, 1)
    pool.wait_ge(pool_consts, 2)
    nc.gpsimd.affine_select(out=ident[:, :], in_=ident[:, :], compare_op=ALU.not_equal, fill=1.0, base=0,
                            pattern=[[-1, P]], channel_multiplier=1).then_inc(pool_consts, 1)


def constants_pe(nc, v, pe):
    pe.wait_ge(v["consts_in"], 48)
    pe.wait_ge(v["pool_consts"], 3)
    nc.tensor.matmul(v["ps_a"][:, 0:B], v["ones"][:, :], v["cond_t"][:, :], start=True,
                     stop=True).then_inc(v["cond_sum"], 1)


def constants_dve(nc, v, dve, late):
    tf, dec, dec0, osc, osc2, setup_dve = (v[n] for n in "tf dec dec0 osc osc2 setup_dve".split())
    EARLY = 4

    def done(ins, wait=None):
        ins.then_inc(setup_dve, 1)
        if wait:
            dve.wait_ge(setup_dve, wait)

    def decay(b):
        return nc.vector.tensor_scalar(dec[:, b, :], dec0[:, 1, :], tf[:, 3, b:b + 1], None, ALU.mult)

    if not late:
        dve.wait_ge(v["setup_exp"], 3)
        done(nc.vector.tensor_scalar(tf[:, 1, :], tf[:, 0, :], 1.0, None, ALU.add), 1)
        done(nc.vector.reciprocal(tf[:, 2, :], tf[:, 1, :]), 2)
        done(nc.vector.tensor_scalar(tf[:, 3, :], tf[:, 2, :], 0.5, 0.5, ALU.mult, ALU.add), 3)
        done(decay(0), EARLY)
    else:
        done(nc.vector.tensor_scalar(osc2[:, :], tf[:, 2, :], -0.2, -0.8, ALU.mult, ALU.add))
        done(nc.vector.tensor_scalar(osc[:, :], tf[:, 2, :], -0.1, -0.4, ALU.mult, ALU.add))
        for b in range(1, B):
            done(decay(b), EARLY + 1 + B if b == B - 1 else None)


def constants_lut(nc, v, dve):
    lut_d, lut_in, lut_diff = v["lut_d"], v["lut_in"], v["lut_diff"]
    dve.wait_ge(v["late_consts_in"], 64)
    pair = lut_in[:, :].rearrange("p (n two) -> p n two", two=2)
    nc.vector.tensor_tensor(lut_d[:, :], pair[:, :, 1], pair[:, :, 0], ALU.subtract).then_inc(lut_diff, 1)
    dve.wait_ge(lut_diff, 1)
    nc.vector.tensor_scalar(lut_d[:, :], lut_d[:, :], 1.0 / BIT0, None, ALU.mult)


def kernel(**inputs):
    import numpy as np
    import concourse.bacc as bacc
    from concourse.bass_utils import run_bass_kernel_spmd

    a = {n: np.asarray(v) for n, v in inputs.items()}

    def columns(v):
        return v.reshape(CC, P).T

    def chunked(idx):
        idx = np.pad(idx, ((0, FJ * P - F), (0, 0)))
        return idx.reshape(FJ, P, CC, P).transpose(0, 3, 2, 1).reshape(FJ, P, CC * P)

    down = np.pad(a["L1_ffn_down_idx"], ((0, 0), (0, FJ * P - F))).T.reshape(FJ, P, C)
    idx = np.concatenate([chunked(a["L1_ffn_gate_idx"]), chunked(a["L1_ffn_up_idx"]), down], axis=2)
    idx = idx.reshape(FJ, P, WJ // SB, SB).transpose(0, 2, 1, 3).reshape(NS, P, SB)
    idx = np.pad(idx, ((0, 2), (0, 0), (0, 0)))
    arrays = {
        "x": a["x"].transpose(0, 2, 1).reshape(B, CC, P, T),
        "k": np.pad(a["fside_BxSxS_0"].transpose(0, 2, 1).reshape(B, CC, P, T), ((0, 1), (0, 0), (0, 0), (0, 0))),
        "cond": a["cond_512"].T,
        "w": np.concatenate([columns(a["L0_cond_w"]), columns(a["L1_cond_w"])], axis=1),
        "u": np.concatenate([columns(a["L0_cond_u"]), columns(a["L1_cond_u"])], axis=1),
        "router_w": a["L0_ffn_router_weight"].T.reshape(CC, P, E).transpose(1, 0, 2),
        "router_b": a["L0_ffn_router_bias"].reshape(1, E),
        "expert_b": a["L0_ffn_expert_bias"],
        "lut": a["L1_ffn_lut"].reshape(1, 16),
        "idx": idx,
    }
    arrays = {n: np.ascontiguousarray(v) for n, v in arrays.items()}
    nc = bacc.Bacc("TRN2", target_bir_lowering=False, num_devices=1, dynamic_dma_scratch_size=1024)
    aps = {n: nc.dram_tensor(f"in_{n}", v.shape, mybir.dt.from_np(v.dtype), kind="ExternalInput").ap()
           for n, v in arrays.items()}
    y = nc.dram_tensor("y", (B, CC, P, T), F32, kind="ExternalOutput").ap()
    build(nc, y=y, **aps)
    r = run_bass_kernel_spmd(nc, [{f"in_{n}": v for n, v in arrays.items()}], core_ids=[0])
    out = r.results[0]["y"]
    return np.ascontiguousarray(out.reshape(B, C, T).transpose(0, 2, 1))
```
